# Optimizing a Trainium2 kernel written in Bass

```python
import numpy as np
import jax
import jax.numpy as jnp

def _softmax(x, axis=-1):
    return jax.nn.softmax(x, axis=axis)

def _gelu(x):
    return jax.nn.gelu(x, approximate=True)

def _silu(x):
    return jax.nn.silu(x)

def _sigmoid(x):
    return jax.nn.sigmoid(x)

def _layernorm(x, axis=-1, eps=1e-05):
    m = jnp.mean(x, axis=axis, keepdims=True)
    v = jnp.var(x, axis=axis, keepdims=True)
    return (x - m) / jnp.sqrt(v + eps)

def _scatter_add(tgt, idx, src, axis=0):
    return tgt.at[idx].add(src)

def _segment_sum(src, seg, n):
    return jax.ops.segment_sum(src, seg, n)
kernel_name = 'mk_xattn_ffn_d1_seqx_r4_91c804'

def setup_inputs(seed: int=0):
    np.random.seed(seed)
    _w = jnp.asarray

    def _rec_inputs():
        import jax
        import jax.numpy as jnp
        _rk = jax.random.key(seed)
        x = -0.0002928 + 1 * jax.random.normal(jax.random.fold_in(_rk, 1), (4, 1024, 256), jnp.float32)
        _lenS = 1024 - jax.random.randint(jax.random.fold_in(_rk, 7), (4,), 0, max(1, 1024 // 4) + 1, jnp.int32)
        _lenS2 = 77 - jax.random.randint(jax.random.fold_in(_rk, 8), (4,), 0, max(1, 77 // 4) + 1, jnp.int32)
        _ctx_1024P = jax.random.normal(jax.random.fold_in(_rk, 11), (4, 16, 256), jnp.float32)
        _ctx_1024c = jax.random.dirichlet(jax.random.fold_in(_rk, 511), 0.3 * jnp.ones((16,), jnp.float32), (4, 77))
        _ctx_1024t = jnp.einsum('bsk,bkd->bsd', _ctx_1024c, _ctx_1024P)
        _ctx_1024t = _ctx_1024t * jax.lax.rsqrt(jnp.mean(jnp.square(_ctx_1024t)) + 1e-12) * 0.953939
        ctx_1024 = -1.39393e-06 + 0.999914 * (_ctx_1024t + 0.3 * jax.random.normal(jax.random.fold_in(_rk, 611), (4, 77, 256), jnp.float32))
        _validS = jnp.arange(1024)[None, :] < _lenS[:, None]
        _validS2 = jnp.arange(77)[None, :] < _lenS2[:, None]
        _causal = jnp.tril(jnp.ones((1024, 1024), dtype=bool))
        mask_SxS2_ik0 = jnp.where(jnp.broadcast_to(_validS2[0:1, :], (1024, 77)), 0, 1).astype(jnp.int32)
        return (x, ctx_1024, mask_SxS2_ik0)
    x, ctx_1024, mask_SxS2_ik0 = _rec_inputs()

    def _L0_xattn_setup():
        import jax, jax.numpy as jnp
        import numpy as np
        D_MODEL = 256
        N_HEAD = 16
        B, S = (2, 512)
        key = jax.random.key(seed)
        ks = jax.random.split(key, 12)
        std = 1.0 / np.sqrt(D_MODEL)
        inp = {'q': jax.random.normal(ks[0], (B, S, D_MODEL), jnp.float32), 'k': jax.random.normal(ks[1], (B, S, D_MODEL), jnp.float32), 'v': jax.random.normal(ks[2], (B, S, D_MODEL), jnp.float32), 'mask': jnp.tril(jnp.ones((S, S), jnp.int32)), 'Wq': jax.random.normal(ks[3], (D_MODEL, D_MODEL), jnp.float32) * std, 'bq': jax.random.normal(ks[4], (D_MODEL,), jnp.float32) * std, 'Wk': jax.random.normal(ks[5], (D_MODEL, D_MODEL), jnp.float32) * std, 'bk': jax.random.normal(ks[6], (D_MODEL,), jnp.float32) * std, 'Wv': jax.random.normal(ks[7], (D_MODEL, D_MODEL), jnp.float32) * std, 'bv': jax.random.normal(ks[8], (D_MODEL,), jnp.float32) * std, 'Wo': jax.random.normal(ks[9], (D_MODEL, D_MODEL), jnp.float32) * std, 'bo': jax.random.normal(ks[10], (D_MODEL,), jnp.float32) * std}
        return inp
    _L0_xattn_all = _L0_xattn_setup()
    _L0_xattn_in = {k: v for k, v in _L0_xattn_all.items() if k in ('Wq', 'bq', 'Wk', 'bk', 'Wv', 'bv', 'Wo', 'bo')}
    del _L0_xattn_all

    def _L0_ffn_setup():
        import jax, jax.numpy as jnp
        import numpy as np
        H = 256
        I = 128
        E = 32
        TOP_K = 6
        N_GROUP = 8
        TOPK_GROUP = 4
        SCALE = 2.5
        N_SHARED = 2
        SI = I * N_SHARED
        B, S = (2, 256)
        key = jax.random.key(seed)
        ks = jax.random.split(key, 8)
        x = jax.random.normal(ks[0], (B, S, H), jnp.float32)
        gate_weight = jax.random.normal(ks[1], (E, H), jnp.float32) * 0.02
        e_score_correction_bias = jax.random.normal(ks[2], (E,), jnp.float32) * 0.01
        experts_gate_up = jax.random.normal(ks[3], (E, 2 * I, H), jnp.float32) * 0.02
        experts_down = jax.random.normal(ks[4], (E, H, I), jnp.float32) * 0.02
        shared_gate_w = jax.random.normal(ks[5], (SI, H), jnp.float32) * 0.02
        shared_up_w = jax.random.normal(ks[6], (SI, H), jnp.float32) * 0.02
        shared_down_w = jax.random.normal(ks[7], (H, SI), jnp.float32) * 0.02
        return {'x': x, 'gate_weight': gate_weight, 'e_score_correction_bias': e_score_correction_bias, 'experts_gate_up': experts_gate_up, 'experts_down': experts_down, 'shared_gate_w': shared_gate_w, 'shared_up_w': shared_up_w, 'shared_down_w': shared_down_w}
    _L0_ffn_all = _L0_ffn_setup()
    _L0_ffn_in = {k: v for k, v in _L0_ffn_all.items() if k in ('gate_weight', 'e_score_correction_bias', 'experts_gate_up', 'experts_down', 'shared_gate_w', 'shared_up_w', 'shared_down_w')}
    del _L0_ffn_all
    return {'x': x, 'ctx_1024': ctx_1024, 'mask_SxS2_ik0': mask_SxS2_ik0, 'L0_xattn_Wq': _L0_xattn_in['Wq'], 'L0_xattn_bq': _L0_xattn_in['bq'], 'L0_xattn_Wk': _L0_xattn_in['Wk'], 'L0_xattn_bk': _L0_xattn_in['bk'], 'L0_xattn_Wv': _L0_xattn_in['Wv'], 'L0_xattn_bv': _L0_xattn_in['bv'], 'L0_xattn_Wo': _L0_xattn_in['Wo'], 'L0_xattn_bo': _L0_xattn_in['bo'], 'L0_ffn_gate_weight': _L0_ffn_in['gate_weight'], 'L0_ffn_e_score_correction_bias': _L0_ffn_in['e_score_correction_bias'], 'L0_ffn_experts_gate_up': _L0_ffn_in['experts_gate_up'], 'L0_ffn_experts_down': _L0_ffn_in['experts_down'], 'L0_ffn_shared_gate_w': _L0_ffn_in['shared_gate_w'], 'L0_ffn_shared_up_w': _L0_ffn_in['shared_up_w'], 'L0_ffn_shared_down_w': _L0_ffn_in['shared_down_w']}

def reference(x, ctx_1024, mask_SxS2_ik0, L0_xattn_Wq, L0_xattn_bq, L0_xattn_Wk, L0_xattn_bk, L0_xattn_Wv, L0_xattn_bv, L0_xattn_Wo, L0_xattn_bo, L0_ffn_gate_weight, L0_ffn_e_score_correction_bias, L0_ffn_experts_gate_up, L0_ffn_experts_down, L0_ffn_shared_gate_w, L0_ffn_shared_up_w, L0_ffn_shared_down_w):
    import jax
    import jax.numpy as jnp

    def _L0_xattn_ref(q, k, v, mask, Wq, bq, Wk, bk, Wv, bv, Wo, bo):
        import jax, jax.numpy as jnp
        import numpy as np
        D_MODEL = 256
        N_HEAD = 16
        B, S = (2, 512)
        H = N_HEAD
        b, s, d = q.shape
        dh = d // H

        def split_heads(x, W, bias):
            y = x @ W.T + bias
            return y.reshape(b, -1, H, dh).transpose(2, 0, 1, 3)
        qh = split_heads(q, Wq, bq)
        kh = split_heads(k, Wk, bk)
        vh = split_heads(v, Wv, bv)
        scale = 1.0 / jnp.sqrt(jnp.float32(dh))
        scores = jnp.einsum('hbsd,hbtd->hbst', qh, kh) * scale
        scores = jnp.where(mask == 0, jnp.float32(-1000000000.0), scores)
        attn = jax.nn.softmax(scores, axis=-1)
        out = jnp.einsum('hbst,hbtd->hbsd', attn, vh)
        out = out.transpose(1, 2, 0, 3).reshape(b, s, d)
        return out @ Wo.T + bo

    def _L0_ffn_ref(x, gate_weight, e_score_correction_bias, experts_gate_up, experts_down, shared_gate_w, shared_up_w, shared_down_w):
        import jax, jax.numpy as jnp
        import numpy as np
        H = 256
        I = 128
        E = 32
        TOP_K = 6
        N_GROUP = 8
        TOPK_GROUP = 4
        SCALE = 2.5
        N_SHARED = 2
        SI = I * N_SHARED
        B, S = (2, 256)
        b, s, h = x.shape
        xf = x.reshape(-1, h)
        T = xf.shape[0]
        logits = xf.astype(jnp.float32) @ gate_weight.astype(jnp.float32).T
        scores = jax.nn.sigmoid(logits)
        sfc = scores + e_score_correction_bias[None, :]
        gs = E // N_GROUP
        group_scores = sfc.reshape(T, N_GROUP, gs).max(axis=-1)
        _, gidx = jax.lax.top_k(group_scores, TOPK_GROUP)
        gmask = jnp.zeros((T, N_GROUP), bool).at[jnp.arange(T)[:, None], gidx].set(True)
        smask = jnp.repeat(gmask, gs, axis=1)
        masked = jnp.where(smask, sfc, 0.0)
        _, topk_idx = jax.lax.top_k(masked, TOP_K)
        tw = jnp.take_along_axis(scores, topk_idx, axis=1)
        tw = tw / (tw.sum(-1, keepdims=True) + 1e-20)
        tw = (tw * SCALE).astype(xf.dtype)
        combine = jnp.zeros((T, E), xf.dtype).at[jnp.arange(T)[:, None], topk_idx].add(tw)

        def expert_step(acc, inp):
            gu, dn, c = inp
            g = xf @ gu[:I].T
            u = xf @ gu[I:].T
            o = jax.nn.silu(g) * u @ dn.T
            return (acc + c[:, None] * o, None)
        routed, _ = jax.lax.scan(expert_step, jnp.zeros_like(xf), (experts_gate_up, experts_down, combine.T))
        sh = jax.nn.silu(xf @ shared_gate_w.T) * (xf @ shared_up_w.T)
        shared_out = sh @ shared_down_w.T
        return (routed + shared_out).reshape(b, s, h)
    x = x + _L0_xattn_ref(_layernorm(x, axis=-1), ctx_1024, ctx_1024, mask_SxS2_ik0, L0_xattn_Wq, L0_xattn_bq, L0_xattn_Wk, L0_xattn_bk, L0_xattn_Wv, L0_xattn_bv, L0_xattn_Wo, L0_xattn_bo)
    x = x + _L0_ffn_ref(_layernorm(x, axis=-1), L0_ffn_gate_weight, L0_ffn_e_score_correction_bias, L0_ffn_experts_gate_up, L0_ffn_experts_down, L0_ffn_shared_gate_w, L0_ffn_shared_up_w, L0_ffn_shared_down_w)
    return x

_drawn_inputs = setup_inputs


def setup_inputs(seed=0):
    import zlib

    import numpy as np

    out = dict(_drawn_inputs(seed))
    spreads = {}
    factors = {'L0_xattn_bq': 3.331,
     'L0_xattn_bk': 8.0,
     'L0_ffn_gate_weight': 6.391,
     'L0_ffn_e_score_correction_bias': 8.0,
     'L0_ffn_experts_gate_up': 5.826,
     'L0_ffn_experts_down': 5.798,
     'L0_ffn_shared_gate_w': 4.235,
     'L0_ffn_shared_up_w': 4.153,
     'L0_ffn_shared_down_w': 4.165}
    for name, (base, spread) in spreads.items():
        noise = np.random.default_rng([zlib.crc32(name.encode()), seed]).standard_normal(out[name].shape)
        drawn = base * np.exp(spread * noise) if base else spread * noise
        out[name] = jnp.asarray(drawn.astype(out[name].dtype))
    for name, factor in factors.items():
        out[name] = (out[name] * factor).astype(out[name].dtype)
    return out
```

```python
import concourse.bass as bass
from concourse import mybir
from contextlib import ExitStack
import numpy as np

B, S, D = 4, 1024, 256
C, H, DH = 77, 16, 16
E, I, TOPK = 32, 128, 6
NG, GS, TOPG = 8, 4, 4
SI = 256
P = 128
KT = D // P
NT = B * S // P
SB = S // P
ROUTE_SCALE = 2.5
EPS = 1e-5
HC = H * C
NCH = -(-HC // P)
PV = DH + 1
HCOLS = 4 * C
MASKED = -float(2 ** 60)
ROW = D + E + 1
REGION = B * S + P
PAD_ROW = E * REGION
NTB = -(-((B * S * TOPK + E * (P - 1)) // P) // 8) * 8
R_ACC = 4
RX = 8
W_LOADS = 5 + KT + 3 * (KT + 1) + 3
UA, UB = 4, 8


def chunk_head(c):
    return min(P * c // C, H - 3)


CONST = {}


def _const_layout():
    at = 0
    for name, n in (("ident", P), ("submask", 2), ("vmask", NCH * 3), ("iota", E), ("region", E),
                    ("jtile", 2), ("third", 3), ("half_neg", E), ("tri", P), ("ones", P), ("rep", HCOLS)):
        CONST[name] = (at, at + n)
        at += n
    return at


NCONST = _const_layout()


def constants():
    c = np.zeros((P, NCONST), np.float32)

    def put(name, a):
        lo, hi = CONST[name]
        c[:, lo:hi] = a
    p = np.arange(P)[:, None]
    put("ident", np.eye(P))
    put("submask", (p % 32) // DH == np.arange(2)[None])
    vm = np.zeros((P, NCH, 3))
    for ch in range(NCH):
        row = ch * P + np.arange(P)
        for j in range(3):
            vm[:, ch, j] = (row // C == chunk_head(ch) + j) & (row < HC)
    put("vmask", vm.reshape(P, -1))
    put("iota", np.arange(E)[None])
    put("region", REGION * np.arange(E)[None])
    put("jtile", p + P * np.arange(2)[None])
    put("third", p == np.arange(3)[None])
    put("half_neg", -0.5)
    put("tri", p < np.arange(P)[None])
    put("ones", 1.0)
    put("rep", p == np.arange(HCOLS)[None] % C)
    ids = np.zeros((P, NT + 1), np.int32)
    t = np.arange(NT)[None]
    ids[:, :NT] = (t % B) * S + (t // B) * P + p
    ids[:, NT] = B * S + p[:, 0]
    return c, ids


def build(nc, x, mask, wq, wk, wv, wo, bqk, bvo, ctx_t, gate_w, gate_b, egu, edn, sgu, sdn, const_in, ids_in, out):
    fp32, bf16, i32, u32 = mybir.dt.float32, mybir.dt.bfloat16, mybir.dt.int32, mybir.dt.uint32
    ALU, ACT, AX = mybir.AluOpType, mybir.ActivationFunctionType, mybir.AxisListType

    rows = nc.dram_tensor("rows", (PAD_ROW + P, ROW), fp32, kind="Internal").ap()
    acc = [nc.dram_tensor(f"acc{r}", (REGION, D), fp32, kind="Internal").ap() for r in range(R_ACC)]

    with ExitStack() as ctx:
        def sb(name, shape, dt=fp32):
            return ctx.enter_context(nc.sbuf_tensor(name, shape, dt))

        S_ = {}

        def sem(name):
            S_[name] = ctx.enter_context(nc.semaphore(name))
            return S_[name]

        wgu = sb("wgu", [P, E * KT * 2 * I])
        wdn = sb("wdn", [P, E * D])
        wsgu = sb("wsgu", [P, KT, 2 * SI])
        wsdn = sb("wsdn", [P, KT, D])
        wq_sb = sb("wq_sb", [P, KT, D])
        wo_sb = sb("wo_sb", [P, KT, D])
        wg_sb = sb("wg_sb", [P, KT, E])
        kbd = sb("kbd", [P, 2, B, 2 * C])
        vbd = sb("vbd", [P, B, NCH, 3, PV])
        maskb = sb("maskb", [C, S], bf16)
        repb = sb("repb", [C, HCOLS], bf16)
        trib = sb("trib", [P, P], bf16)
        onesb = sb("onesb", [P, P], bf16)
        cst = sb("cst", [P, NCONST])
        ids = sb("ids", [P, NT + 1], i32)
        bias_qk = sb("bias_qk", [P, 4])
        bo3 = sb("bo3", [3, D], bf16)
        gbias = sb("gbias", [P, E])
        store = sb("store", [P, NT * D])
        stats1 = sb("stats1", [P, NT, 6])
        mean1 = sb("mean1", [P, NT])
        rstd1 = sb("rstd1", [P, NT])
        tmp1 = sb("tmp1", [P, 2, NT])
        xn = sb("xn", [P, 2, D])
        xnT = sb("xnT", [P, 2, D])
        qT = sb("qT", [P, 2, D])
        mx = sb("mx", [P, H])
        probs = sb("probs", [P, 2, NCH * P])
        pT = sb("pT", [P, NCH, P])
        rsum = sb("rsum", [P, H])
        o = sb("o", [P, 2, D])
        oT = sb("oT", [P, 2, D])
        x1 = sb("x1", [P, 2, D])
        stats2 = sb("stats2", [P, 6])
        mv2 = sb("mv2", [P, 2, 2])
        var2 = sb("var2", [P, 2])
        rstd2 = sb("rstd2", [P, 2])
        rowb = sb("rowb", [P, 4, ROW])
        xn2T = sb("xn2T", [P, 2, D])
        gexp = sb("gexp", [P, 2, E])
        gsum = sb("gsum", [P, E])
        score = sb("score", [P, E])
        sfc = sb("sfc", [P, E])
        gmax = sb("gmax", [P, NG])
        gtop = sb("gtop", [P, 8])
        gidx = sb("gidx", [P, 8], u32)
        ghot = sb("ghot", [P, NG, TOPG])
        gsel = sb("gsel", [P, NG])
        masked = sb("masked", [P, E])
        etop = sb("etop", [P, 8])
        eidx = sb("eidx", [P, 8], u32)
        ehot = sb("ehot", [P, E, TOPK])
        sel = sb("sel", [P, E], bf16)
        selcum = sb("selcum", [P, E], bf16)
        wsel = sb("wsel", [P, E])
        wsum = sb("wsum", [P, 4])
        place = sb("place", [P, E])
        placek = sb("placek", [P, TOPK, E])
        dest = sb("dest", [P, 2, 8], u32)
        padrow = sb("padrow", [P, ROW])
        zeros = sb("zeros", [P, D])
        cnt = sb("cnt", [P, E])
        blocks = sb("blocks", [P, E])
        blkcum = sb("blkcum", [P, E])
        sched = sb("sched", [P, 4])
        sched2 = sb("sched2", [P, 4])
        table = sb("table", [1, 4 * P], i32)
        tails = sb("tails", [1, E], i32)

        def carve(base, at, shape):
            n = int(np.prod(shape[1:]))
            v = base[:, at:at + n]
            names = "abcd"[:len(shape) - 1]
            if len(shape) > 2:
                v = v.rearrange("p (%s) -> p %s" % (" ".join(names), " ".join(names)),
                                **{k: d for k, d in zip(names[1:], shape[2:])})
            return v, at + n
        wk_sb, at = carve(wdn, 0, [P, KT, D])
        wv_sb, at = carve(wdn, at, [P, KT, D])
        ctxT, at = carve(wdn, at, [P, KT, B * C])
        ctx3, at = carve(wdn, at, [P, KT, B, 3 * C])
        bv_row, at = carve(wdn, at, [P, D])
        gb_row, at = carve(wdn, at, [P, E])
        bo_f, at = carve(wdn, at, [P, D])
        bo_r, at = carve(wdn, at, [P, D])
        bo_s, at = carve(wdn, at, [P, D])
        assert at <= E * D
        maskw = wgu[:, 0:S].bitcast(i32)
        bo_p = wgu[:, S:S + 3 * P]

        xe = probs[:, :, :].rearrange("p a b -> p (a b)")[:, 0:RX * ROW].rearrange("p (a b) -> p a b", b=ROW)
        pTf = pT[:, :, :].rearrange("p a b -> p (a b)")
        xeT = xnT
        act = qT[:, :, 0:I]
        hid = o[:, :, 0:I]
        hidT = oT[:, :, 0:I]
        ye = pTf[:, 0:R_ACC * D].rearrange("p (a b) -> p a b", b=D)
        acc_in, at = carve(wgu, 0, [P, 2 * R_ACC, B * D])
        shg, at = carve(wgu, at, [P, 2, B * P])
        shh, at = carve(wgu, at, [P, 4, B * P])
        outb, at = carve(wgu, at, [P, 2, B * D])
        assert at <= E * KT * 2 * I

        bank = [ctx.enter_context(nc.psum_tensor(f"bank{i}", [P, 512], fp32)) for i in range(4, 8)]
        sc_ps = ctx.enter_context(nc.psum_tensor("sc_ps", [P, 4, 512], fp32))
        xT_ps = bank[0][:, 0:D].rearrange("p (k n) -> p k n", k=KT)
        pT_ps = [bank[1], bank[2], bank[1]]
        oT_ps = bank[3][:, 0:D]
        x2T_ps = xT_ps
        q_ps = bank[2][:, 0:D]
        pv_ps = bank[3][:, 0:H * PV]
        y_ps = bank[0][:, 0:D]
        lg_ps = bank[1][:, 0:E]
        rk_ps = bank[2][:, 0:E]
        ps8 = [sc_ps[:, i, :] for i in range(4)] + [b[:, :] for b in bank]

        for name in ("ld_const ld_w ld_gate ld_egu ld_edn ld_mask cst_b k_ps kbd_ready v_ps vbd_ready gb_ps gb_ready "
                     "bo_parts mask_ready repb_ready zero_ready pad_ready pool_go probs_zero setup_read wg_free stats1_ready "
                     "mean1_ready tmp_ready var1_ready "
                     "rstd1_ready sel_zero acc_init pad_init "
                     "xn xT_ps xnT q_ps qT scores score_max score_sub probs pT_ps0 pT_ps1 pT_ps2 pT0 pT1 pT2 pv o_rcp o "
                     "oT_ps oT y_ps x1 stats2 mv2 var2 rstd2 row_id xn2 x2T_ps xn2T logits gate_exp "
                     "gate_add score sfc gmax gtop gidx ghot gsel masked etop eidx ehot sel wsel wsum_e wsum_r row_w "
                     "rank place placek dest selcum "
                     "counts cnt sch_a sch_b sch_c sch_d sch_e sch_ps table tail_rows tails_st "
                     "xeT_ps xeT gu_ps act hid hidT_ps hidT ye_ps ye "
                     "sg_ps shg shh sy_ps acc_sum outb out_st").split():
            sem(name)
        ld_x = [sem(f"ld_x{i}") for i in range(SB)]
        x1_st = [sem(f"x1_st{i}") for i in range(2)]
        xn2T_st = [sem(f"xn2T_st{i}") for i in range(2)]
        scat = [sem(f"scat{i}") for i in range(4)]
        ld_xe = [sem(f"ld_xe{i}") for i in range(RX)]
        acc_add = [sem(f"acc_add{i}") for i in range(R_ACC)]
        ld_acc = [sem(f"ld_acc{i}") for i in range(2)]

        def need(eng, name, t, per=1):
            eng.wait_ge(S_[name], (t + 1) * per)

        def need_apart(eng, name, t):
            eng.wait_ge(S_[name], 1)
            need(eng, name, t)

        def freed(eng, name, t, ring, per=1):
            if isinstance(t, int) and t < ring:
                return
            eng.wait_ge(S_[name], (t - (ring - 1)) * per)

        def stored(eng, sems, m, s):
            n = len(sems)
            per = 16 * TOPK if n == 4 else 16
            count = s * (UA // n) + m // n
            if not (isinstance(count, int) and count == 0):
                eng.wait_ge(sems[m % n], count * per)

        def dest_free(eng, m, s):
            count = s + 1 if m >= 2 else s
            if not (isinstance(count, int) and count == 0):
                eng.wait_ge(scat[(m + 2) % 4], count * 16 * TOPK)

        def read_out(eng, name, t, ahead):
            n = t + ahead + 1
            if not isinstance(n, int):
                eng.wait_ge(S_[name], n)
            elif n > 0:
                eng.wait_ge(S_[name], min(n, NT))

        def const(name):
            lo, hi = CONST[name]
            return cst[:, lo:hi]

        block = ctx.enter_context(nc.Block())

        LEAD, LAG = 1, 5
        FIRST, TRIPS = 7, (NT - LEAD - 7) // UA
        LAST = FIRST + UA * TRIPS

        def over_tiles(eng, step):
            def fixed(n):
                def tile(lag):
                    t = n - lag
                    return (t, t % UA, t // B) if 0 <= t < NT else None
                return tile
            for n in range(-LEAD, FIRST):
                step(fixed(n))
            with eng.Fori(0, TRIPS) as k:
                for u in range(UA):
                    def tile(lag, u=u):
                        base = FIRST + u - lag
                        return (k * UA + base, base % UA, k + base // B)
                    step(tile)
            for n in range(LAST, NT + LAG):
                step(fixed(n))

        def at_tile(tile, lag, stage):
            got = tile(lag)
            if got is not None:
                stage(*got)

        BFIRST, BTRIPS = UB - 1, (NTB - UB) // UB
        BLAST = BFIRST + UB * BTRIPS

        def over_expert_tiles(eng, step):
            def fixed(n):
                def tile(lag):
                    j = n - lag
                    return (j, j % UB, j // UB) if 0 <= j < NTB else None
                return tile
            for n in range(-1, BFIRST):
                step(fixed(n))
            with eng.Fori(0, BTRIPS) as k:
                for u in range(UB):
                    def tile(lag, u=u):
                        base = BFIRST + u - lag
                        return (k * UB + base, base % UB, k + base // UB)
                    step(tile)
            for n in range(BLAST, NTB + 2):
                step(fixed(n))

        @block.sync
        def _(sp):
            sp.dma_start(cst[:, :], const_in[:, :]).then_inc(S_["ld_const"], 16)
            for s in range(SB):
                sp.dma_start(store[:, s * B * D:(s + 1) * B * D].rearrange("p (b d) -> p b d", b=B),
                             x[:, s * P:(s + 1) * P, :].rearrange("b p d -> p b d")).then_inc(ld_x[s], 16)
            need(sp, "zero_ready", 0)
            for r in range(R_ACC):
                n0 = B * S if r == 0 else 0
                n = (REGION - n0) // P
                sp.dma_start(acc[r][n0:REGION, :].rearrange("(n p) d -> p n d", p=P),
                             zeros[:, :].unsqueeze(1).broadcast_to([P, n, D])).then_inc(S_["acc_init"], 16)
            need(sp, "pad_ready", 0)
            sp.dma_start(rows[PAD_ROW:PAD_ROW + P, :], padrow[:, :]).then_inc(S_["tails_st"], 16)
            sp.dma_start(wsgu[:, :, :], sgu.rearrange("(k p) n -> p k n", p=P)).then_inc(S_["ld_egu"], 16)
            sp.dma_start(wsdn[:, :, :], sdn.rearrange("(k p) n -> p k n", p=P)).then_inc(S_["ld_egu"], 16)
            need(sp, "wg_free", 0)
            for e0 in range(0, E, 8):
                sp.dma_start(wgu[:, e0 * 512:(e0 + 8) * 512].rearrange("p (e k n) -> p e k n", e=8, k=KT),
                             egu[e0:e0 + 8].rearrange("e (k p) n -> p e k n", p=P)).then_inc(S_["ld_egu"], 16)
            sp.wait_ge(S_["kbd_ready"], 2)
            need(sp, "vbd_ready", 0, B)
            need(sp, "gb_ready", 0)
            sp.wait_ge(S_["bo_parts"], 9)
            for e0 in range(0, E, 8):
                sp.dma_start(wdn[:, e0 * D:(e0 + 8) * D].rearrange("p (e n) -> p e n", e=8),
                             edn[e0:e0 + 8].rearrange("e p n -> p e n")).then_inc(S_["ld_edn"], 16)

            def st_x1(t, m, s):
                need(sp, "x1", t)
                sp.dma_start(acc[0][bass.ds(s * P + (m * S), P), :], x1[:, m % 2, :]).then_inc(x1_st[m % 2], 16)

            def st_xn2T(t, m, s):
                need(sp, "xn2T", t)
                sp.dma_start(store[:, bass.ds(t * D, D)], xn2T[:, m % 2, :]).then_inc(xn2T_st[m % 2], 16)

            def step(tile):
                at_tile(tile, 2, st_x1)
                at_tile(tile, 3, st_xn2T)
            over_tiles(sp, step)

            need(sp, "tail_rows", 0)
            with sp.Fori(0, E) as e:
                r = sp.value_load(tails[0:1, bass.ds(e, 1)], min_val=0, max_val=PAD_ROW - P)
                sp.dma_start(rows[bass.ds(r, P), :], padrow[:, :]).then_inc(S_["tails_st"], 16)
            need(sp, "table", 0)
            sp.wait_ge(S_["tails_st"], 16 * (E + 1))
            for one in scat:
                sp.wait_ge(one, 16 * TOPK * NT // 4)

            def ld_tile(j, m):
                r = sp.value_load(table[0:1, bass.ds(j + 2 * P, 1)], min_val=0, max_val=PAD_ROW)
                sp.dma_start(xe[:, m, :], rows[bass.ds(r, P), :]).then_inc(ld_xe[m], 16)
            for j in range(RX):
                ld_tile(j, j)
            with sp.Fori(1, NTB // RX) as k:
                for u in range(RX):
                    sp.wait_ge(acc_add[u % R_ACC], (k * 2 - 1 + u // R_ACC) * 16)
                    ld_tile(k * RX + u, u)

            for r in range(R_ACC):
                sp.wait_ge(acc_add[r], 16 * (NTB // R_ACC))
            need(sp, "gu_ps", NTB - 1)

            def ld_accs(s, m):
                for r in range(R_ACC):
                    sp.dma_start(acc_in[:, m * R_ACC + r, :].rearrange("p (b d) -> p b d", b=B),
                                 acc[r][0:B * S, :].rearrange("(b q) d -> q b d", b=B)[bass.ds(s * P, P), :, :]
                                 ).then_inc(ld_acc[m], 16)

            def st_out(s, m):
                need(sp, "outb", s, B)
                sp.dma_start(out.rearrange("b q d -> q b d")[bass.ds(s * P, P), :, :],
                             outb[:, m, :].rearrange("p (b d) -> p b d", b=B)).then_inc(S_["out_st"], 16)
            ld_accs(0, 0)
            ld_accs(1, 1)
            for s in range(SB):
                st_out(s, s % 2)
                if s + 2 < SB:
                    need(sp, "acc_sum", s, R_ACC - 1)
                    ld_accs(s + 2, s % 2)
            sp.wait_ge(S_["out_st"], 16 * SB)

        @block.gpsimd
        def _(pool):
            pool.memset(zeros[:, :], 0.0).then_inc(S_["zero_ready"], 1)
            pool.memset(padrow[:, :], 0.0).then_inc(S_["pad_init"], 1)
            pool.memset(probs[:, :, HC:NCH * P], 0.0).then_inc(S_["probs_zero"], 1)
            pool.memset(selcum[:, :], 0.0).then_inc(S_["selcum"], 1)
            pool.wait_ge(S_["ld_const"], 32)
            pool.wait_ge(S_["pad_init"], 1)
            pool.tensor_copy(padrow[:, ROW - 1:ROW].bitcast(i32), ids[:, NT:NT + 1]).then_inc(S_["pad_ready"], 1)
            need(pool, "var1_ready", 0)
            pool.tensor_tensor(rstd1[:, :], tmp1[:, 0, :], const("half_neg"), ALU.pow).then_inc(S_["rstd1_ready"], 1)

            def scatter(t, m, s):
                need(pool, "dest", t)
                need(pool, "row_id", t)
                pool.sem_inc(S_["pool_go"], 1)
                pool.wait_ge(S_["pool_go"], 1)
                for k in range(TOPK):
                    pool.indirect_dma_start(rows[:, :], bass.IndirectOffsetOnAxis(ap=dest[:, m % 2, k:k + 1], axis=0),
                                            rowb[:, m, :], None).then_inc(scat[m], 16)

            def ids_and_rstd2(t, m, s):
                stored(pool, scat, m, s)
                pool.tensor_copy(rowb[:, m, ROW - 1:ROW].bitcast(i32), ids[:, bass.ds(t, 1)]).then_inc(S_["row_id"], 1)
                need(pool, "var2", t)
                freed(pool, "xn2", t, 2)
                pool.tensor_tensor(rstd2[:, m % 2:m % 2 + 1], var2[:, m % 2:m % 2 + 1], const("half_neg")[:, 0:1],
                                   ALU.pow).then_inc(S_["rstd2"], 1)

            def step(tile):
                at_tile(tile, 5, scatter)
                at_tile(tile, 2, ids_and_rstd2)
            over_tiles(pool, step)

            pool.wait_ge(S_["acc_init"], 16 * R_ACC)
            for one in x1_st:
                pool.wait_ge(one, 16 * NT // 2)

            def add_rows(m):
                pool.indirect_dma_start(acc[m % R_ACC][:, :],
                                        bass.IndirectOffsetOnAxis(ap=xe[:, m, ROW - 1:ROW].bitcast(u32), axis=0),
                                        ye[:, m % R_ACC, :], None, compute_op=ALU.add).then_inc(acc_add[m % R_ACC], 16)
            for j in range(RX):
                need(pool, "ye", j)
                if j >= R_ACC:
                    pool.wait_ge(acc_add[j % R_ACC], 16 * (j // R_ACC))
                add_rows(j)
            with pool.Fori(1, NTB // RX) as k:
                for u in range(RX):
                    need(pool, "ye", k * RX + u)
                    pool.wait_ge(acc_add[u % R_ACC], (k * 2 + u // R_ACC) * 16)
                    pool.sem_inc(S_["pool_go"], 1)
                    pool.wait_ge(S_["pool_go"], 1)
                    add_rows(u)

        @block.scalar
        def _(a):
            a.dma_start(ids[:, :], ids_in[:, :]).then_inc(S_["ld_const"], 16)
            a.dma_start(maskw[0:C, :], mask).then_inc(S_["ld_mask"], 16)
            for dst, src in ((wq_sb, wq), (wk_sb, wk), (wv_sb, wv), (wo_sb, wo), (wg_sb, gate_w)):
                a.dma_start(dst[:, :, :], src.rearrange("(k p) n -> p k n", p=P)).then_inc(S_["ld_w"], 16)
            for k in range(KT):
                a.dma_start(ctxT[:, k, :].rearrange("p (b c) -> p b c", b=B),
                            ctx_t[:, k * P:(k + 1) * P, :].rearrange("b p c -> p b c")).then_inc(S_["ld_w"], 16)
            for i in range(3):
                for k in range(KT):
                    a.dma_start(ctx3[:, k, :, i * C:(i + 1) * C],
                                ctx_t[:, k * P:(k + 1) * P, :].rearrange("b p c -> p b c")).then_inc(S_["ld_w"], 16)
                a.dma_start(bo_f[i:i + 1, :], bvo[1:2, :]).then_inc(S_["ld_w"], 16)
            a.dma_start(bias_qk[:, :], bqk).then_inc(S_["ld_w"], 16)
            a.dma_start(bv_row[0:1, :], bvo[0:1, :]).then_inc(S_["ld_w"], 16)
            a.dma_start(gb_row[0:1, :], gate_b.rearrange("(a n) -> a n", a=1)).then_inc(S_["ld_w"], 16)

            def ev_xT(t, m, s):
                need(a, "xT_ps", t)
                freed(a, "q_ps", t, 2)
                a.activation(xnT[:, m % 2, :].rearrange("p (k n) -> p k n", k=KT), xT_ps, ACT.Copy).then_inc(S_["xnT"], 1)

            def ev_q(t, m, s):
                need(a, "q_ps", t)
                freed(a, "scores", t, 2)
                for h in range(2):
                    last = a.activation(qT[:, m % 2, h * P:(h + 1) * P], q_ps[:, h * P:(h + 1) * P], ACT.Identity,
                                        bias=bias_qk[:, h:h + 1])
                last.then_inc(S_["qT"], 1)

            def exps(t, m, s):
                need(a, "score_sub", t)
                a.activation(probs[:, m % 2, 0:HC], probs[:, m % 2, 0:HC], ACT.Exp,
                             scale=float(DH) ** -0.5).then_inc(S_["probs"], 1)

            def ev_pT(f):
                def stage(t, m, s):
                    need(a, f"pT_ps{f}", t)
                    if f == 0:
                        freed(a, "pv", t, 1)
                    n = min(4, NCH - 4 * f)
                    a.activation(pTf[:, 4 * f * P:(4 * f + n) * P], pT_ps[f][:, 0:n * P], ACT.Copy).then_inc(S_[f"pT{f}"], 1)
                return stage

            def ev_oT(t, m, s):
                need(a, "oT_ps", t)
                freed(a, "y_ps", t, 2)
                a.activation(oT[:, m % 2, :], oT_ps, ACT.Copy).then_inc(S_["oT"], 1)

            def ev_x2T(t, m, s):
                need(a, "x2T_ps", t)
                freed(a, "logits", t, 2)
                stored(a, xn2T_st, m, s)
                a.activation(xn2T[:, m % 2, :].rearrange("p (k n) -> p k n", k=KT), x2T_ps, ACT.Copy).then_inc(S_["xn2T"], 1)

            def gate_exp(t, m, s):
                need(a, "logits", t)
                freed(a, "gate_add", t, 2)
                a.activation(gexp[:, m % 2, :], lg_ps, ACT.Exp, scale=-1.0).then_inc(S_["gate_exp"], 1)

            def step(tile):
                at_tile(tile, -1, ev_xT)
                at_tile(tile, 1, ev_pT(0))
                at_tile(tile, 1, ev_pT(1))
                at_tile(tile, 2, ev_oT)
                at_tile(tile, 3, ev_x2T)
                at_tile(tile, 1, ev_pT(2))
                at_tile(tile, -1, ev_q)
                at_tile(tile, 3, gate_exp)
                at_tile(tile, 0, exps)
            over_tiles(a, step)

            def ev_xeT(j, m, q):
                need(a, "xeT_ps", j)
                freed(a, "gu_ps", j, 2)
                a.activation(xeT[:, m % 2, :], ps8[m % 2][:, 0:D], ACT.Copy).then_inc(S_["xeT"], 1)

            def silu(j, m, q):
                need(a, "gu_ps", j)
                freed(a, "hid", j, 2)
                a.activation(act[:, m % 2, :], ps8[2 + m % 2][:, 0:I], ACT.Silu).then_inc(S_["act"], 1)

            def estep(tile):
                at_tile(tile, 0, silu)
                at_tile(tile, -1, ev_xeT)
            over_expert_tiles(a, estep)

            for s in range(SB):
                for h in range(2):
                    a.wait_ge(S_["sg_ps"], 2 * s + h + 1)
                    if s >= 1:
                        a.wait_ge(S_["shh"], 2 * (s - 1) + h + 1)
                    elif h == 0:
                        need(a, "gu_ps", NTB - 1)
                    a.activation(shg[:, h, :], ps8[2 * h], ACT.Silu).then_inc(S_["shg"], 1)

        @block.tensor
        def _(pe):
            mm = nc.tensor.matmul
            ident = const("ident")

            pe.wait_ge(S_["ld_const"], 32)
            pe.wait_ge(S_["ld_w"], 16 * W_LOADS)
            for h in range(2):
                for k in range(KT):
                    last = mm(ps8[4 + h][:, 0:B * C], wk_sb[:, k, h * P:(h + 1) * P], ctxT[:, k, :],
                              start=k == 0, stop=k == KT - 1)
            last.then_inc(S_["k_ps"], 1)
            ones_row = const("ones")[0:1, :]
            for b in range(B):
                for c in range(NCH):
                    off, n0 = c * P % C, chunk_head(c) * DH
                    cols = ps8[b][:, c * 48:c * 48 + 48]
                    for k in range(KT):
                        mm(cols, ctx3[:, k, b, off:off + P], wv_sb[:, k, n0:n0 + 48], start=k == 0, stop=False)
                    last = mm(cols, ones_row, bv_row[0:1, n0:n0 + 48], start=False, stop=True)
                last.then_inc(S_["v_ps"], 1)
            mm(bank[2][:, 0:E], ones_row, gb_row[0:1, :], start=True, stop=True).then_inc(S_["gb_ps"], 1)
            need(pe, "mask_ready", 0)
            need(pe, "repb_ready", 0, 3)
            need(pe, "gb_ready", 0)
            pe.wait_ge(S_["kbd_ready"], 2)
            pe.wait_ge(S_["vbd_ready"], B)
            pe.wait_ge(S_["bo_parts"], 9)
            need(pe, "probs_zero", 0)

            def tr_x(t, m, s):
                need(pe, "xn", t)
                read_out(pe, "x1", t, -4)
                if isinstance(t, int):
                    read_out(pe, "xnT", t, -1)
                for k in range(KT):
                    last = nc.tensor.transpose(xT_ps[:, k, :], xn[:, m % 2, k * P:(k + 1) * P], ident)
                last.then_inc(S_["xT_ps"], 1)

            def q_proj(t, m, s):
                need(pe, "xnT", t)
                read_out(pe, "pT1", t, -2)
                if isinstance(t, int):
                    read_out(pe, "qT", t, -1)
                for h in range(2):
                    for k in range(KT):
                        last = mm(q_ps[:, h * P:(h + 1) * P], wq_sb[:, k, h * P:(h + 1) * P],
                                  xnT[:, m % 2, k * P:(k + 1) * P], start=k == 0, stop=k == KT - 1)
                last.then_inc(S_["q_ps"], 1)

            def qk(t, m, s):
                need(pe, "qT", t)
                freed(pe, "score_sub", t, 1)
                for r in range(4):
                    mm(sc_ps[:, r, 0:HCOLS], maskb[:, bass.ds(s * P, P)], repb[:, :], start=True, stop=False,
                       skip_group_check=True)
                for h in range(2):
                    for r in range(4):
                        last = mm(sc_ps[:, r, h * 2 * C:(h + 1) * 2 * C],
                                  qT[32 * r:32 * r + 32, m % 2, h * P:(h + 1) * P],
                                  kbd[32 * r:32 * r + 32, h, m, :], start=False, stop=True, skip_group_check=True)
                last.then_inc(S_["scores"], 1)

            def tr_p(f):
                def stage(t, m, s):
                    if f == 0:
                        need(pe, "probs", t)
                        read_out(pe, "gate_exp", t, -3)
                        if isinstance(t, int):
                            read_out(pe, "pT2", t, -1)
                    if f == 1:
                        read_out(pe, "place", t, -4)
                        if isinstance(t, int):
                            read_out(pe, "qT", t, 1)
                            read_out(pe, "pT1", t, -1)
                    if f == 2:
                        read_out(pe, "pT0", t, 0)
                    for c in range(4 * f, min(4 * f + 4, NCH)):
                        last = nc.tensor.transpose(pT_ps[f][:, (c % 4) * P:(c % 4 + 1) * P],
                                                   probs[:, m % 2, c * P:(c + 1) * P], ident)
                    last.then_inc(S_[f"pT_ps{f}"], 1)
                return stage

            def pv(t, m, s):
                read_out(pe, "oT", t, -1)
                for c in range(NCH):
                    if c % 4 == 0:
                        need(pe, f"pT{c // 4}", t)
                    n0 = chunk_head(c) * PV
                    last = mm(pv_ps[:, n0:n0 + 3 * PV], pT[:, c, :], vbd[:, m, c, :, :].rearrange("p a b -> p (a b)"),
                              start=c == 0, stop=c == NCH - 1, skip_group_check=True)
                last.then_inc(S_["pv"], 1)

            def tr_o(t, m, s):
                need(pe, "o", t)
                for k in range(KT):
                    last = nc.tensor.transpose(oT_ps[:, k * P:(k + 1) * P], o[:, m % 2, k * P:(k + 1) * P], ident)
                last.then_inc(S_["oT_ps"], 1)

            def o_proj(t, m, s):
                need(pe, "oT", t)
                read_out(pe, "xn2T", t, -1)
                if isinstance(t, int):
                    read_out(pe, "xnT", t, 3)
                for k in range(KT):
                    mm(y_ps, oT[:, m % 2, k * P:(k + 1) * P], wo_sb[:, k, :], start=k == 0, stop=False)
                mm(y_ps, onesb[0:3, :], bo3[:, :], start=False, stop=True).then_inc(S_["y_ps"], 1)

            def tr_x2(t, m, s):
                need(pe, "xn2", t)
                read_out(pe, "xnT", t, 4)
                for k in range(KT):
                    last = nc.tensor.transpose(x2T_ps[:, k, :], rowb[:, m, k * P:(k + 1) * P], ident)
                last.then_inc(S_["x2T_ps"], 1)

            def gate(t, m, s):
                need(pe, "xn2T", t)
                read_out(pe, "pT2", t, 2)
                if isinstance(t, int):
                    read_out(pe, "gate_exp", t, -1)
                for k in range(KT):
                    last = mm(lg_ps, xn2T[:, m % 2, k * P:(k + 1) * P], wg_sb[:, k, :], start=k == 0, stop=k == KT - 1)
                last.then_inc(S_["logits"], 1)

            def rank(t, m, s):
                need(pe, "sel", t)
                need(pe, "selcum", t)
                read_out(pe, "qT", t, 5)
                if isinstance(t, int):
                    read_out(pe, "pT1", t, 3)
                    read_out(pe, "place", t, -1)
                mm(rk_ps, trib[:, :], sel[:, :], start=True, stop=False)
                mm(rk_ps, onesb[:, :], selcum[:, :], start=False, stop=True).then_inc(S_["rank"], 1)

            def step(tile):
                at_tile(tile, 0, qk)
                at_tile(tile, -1, tr_x)
                at_tile(tile, 1, tr_p(0))
                at_tile(tile, 1, tr_p(1))
                at_tile(tile, 2, tr_o)
                at_tile(tile, 3, tr_x2)
                at_tile(tile, 1, tr_p(2))
                at_tile(tile, -1, q_proj)
                at_tile(tile, 1, pv)
                at_tile(tile, 2, o_proj)
                at_tile(tile, 3, gate)
                at_tile(tile, 4, rank)
            over_tiles(pe, step)

            need(pe, "selcum", NT)
            mm(rk_ps, onesb[:, :], selcum[:, :], start=True, stop=True).then_inc(S_["counts"], 1)
            need(pe, "sch_e", 0)
            for i in range(4):
                last = mm(bank[3][0:1, i * P:(i + 1) * P], sched2[:, i:i + 1], ident, start=True, stop=True)
            last.then_inc(S_["sch_ps"], 1)
            need(pe, "table", 0)
            pe.wait_ge(S_["ld_egu"], 16 * 6)
            pe.wait_ge(S_["ld_edn"], 16 * 4)

            def tr_xe(j, m, q):
                pe.wait_ge(ld_xe[m], (q + 1) * 16)
                freed(pe, "xeT", j, 2)
                for k in range(KT):
                    last = nc.tensor.transpose(ps8[m % 2][:, k * P:(k + 1) * P], xe[:, m, k * P:(k + 1) * P], ident)
                last.then_inc(S_["xeT_ps"], 1)

            def gate_up(j, m, q):
                e = pe.value_load(table[0:1, bass.ds(j, 1)], min_val=0, max_val=E - 1)
                need(pe, "xeT", j)
                freed(pe, "hid", j, 2)
                for k in range(KT):
                    last = mm(ps8[2 + m % 2][:, 0:2 * I], xeT[:, m % 2, k * P:(k + 1) * P],
                              wgu[:, bass.ds(e * 512 + k * 256, 256)], start=k == 0, stop=k == KT - 1)
                last.then_inc(S_["gu_ps"], 1)

            def tr_hid(j, m, q):
                need(pe, "hid", j)
                freed(pe, "hidT", j, 2)
                nc.tensor.transpose(ps8[4 + m % 2][:, 0:I], hid[:, m % 2, :], ident).then_inc(S_["hidT_ps"], 1)

            def down(j, m, q):
                e = pe.value_load(table[0:1, bass.ds(j, 1)], min_val=0, max_val=E - 1)
                need(pe, "hidT", j)
                freed(pe, "ye", j, 2)
                mm(ps8[6 + m % 2][:, 0:D], hidT[:, m % 2, :], wdn[:, bass.ds(e * D, D)], start=True,
                   stop=True).then_inc(S_["ye_ps"], 1)

            def estep(tile):
                at_tile(tile, 0, gate_up)
                at_tile(tile, 1, tr_hid)
                at_tile(tile, 2, down)
                at_tile(tile, -1, tr_xe)
            over_expert_tiles(pe, estep)

            for one in xn2T_st:
                pe.wait_ge(one, 16 * NT // 2)

            def s_up(s):
                xs = store[:, s * B * D:(s + 1) * B * D].rearrange("p (b k n) -> p k b n", b=B, k=KT)
                for h in range(2):
                    if s >= 1:
                        pe.wait_ge(S_["shh"], 2 * (s - 1) + h + 1)
                    elif h == 0:
                        need(pe, "ye", NTB - 1)
                    for g in range(2):
                        for k in range(KT):
                            last = mm(ps8[2 * h + g].rearrange("p (b n) -> p b n", b=B),
                                      wsgu[:, k, g * SI + h * P:g * SI + (h + 1) * P],
                                      xs[:, k, :, :], start=k == 0, stop=k == KT - 1)
                    last.then_inc(S_["sg_ps"], 1)

            def s_down(s):
                need(pe, "shh", s, 2)
                for b in range(B):
                    if s >= 1:
                        pe.wait_ge(S_["outb"], B * (s - 1) + b + 1)
                    for k in range(KT):
                        last = mm(ps8[4 + b][:, 0:D], shh[:, (s % 2) * 2 + k, b * P:(b + 1) * P], wsdn[:, k, :],
                                  start=k == 0, stop=k == KT - 1)
                    last.then_inc(S_["sy_ps"], 1)
            for s in range(SB + 1):
                if s < SB:
                    s_up(s)
                if s >= 1:
                    s_down(s - 1)

        @block.vector
        def _(v):
            tt, ts, red = v.tensor_tensor, v.tensor_scalar, v.tensor_reduce

            for s in range(SB):
                v.wait_ge(ld_x[s], 16)
                for b in range(B):
                    t = s * B + b
                    last = v.bn_stats(stats1[:, t, :], store[:, t * D:(t + 1) * D])
            last.then_inc(S_["stats1_ready"], 1)
            v.wait_ge(S_["stats1_ready"], 1)
            me, mo = stats1[:, :, 1], stats1[:, :, 4]
            ve, vo = stats1[:, :, 2], stats1[:, :, 5]
            tt(mean1[:, :], me, mo, ALU.add).then_inc(S_["mean1_ready"], 1)
            tt(tmp1[:, 0, :], me, mo, ALU.subtract).then_inc(S_["tmp_ready"], 1)
            tt(tmp1[:, 1, :], ve, vo, ALU.add).then_inc(S_["tmp_ready"], 1)
            v.wait_ge(S_["tmp_ready"], 2)
            tt(tmp1[:, 0, :], tmp1[:, 0, :], tmp1[:, 0, :], ALU.mult).then_inc(S_["tmp_ready"], 1)
            ts(tmp1[:, 1, :], tmp1[:, 1, :], 1.0 / D, EPS, ALU.mult, ALU.add).then_inc(S_["tmp_ready"], 1)
            v.wait_ge(S_["mean1_ready"], 1)
            ts(mean1[:, :], mean1[:, :], 0.5, None, ALU.mult).then_inc(S_["mean1_ready"], 1)
            v.wait_ge(S_["tmp_ready"], 4)
            v.scalar_tensor_tensor(tmp1[:, 0, :], tmp1[:, 0, :], 0.25, tmp1[:, 1, :], ALU.mult,
                                   ALU.add).then_inc(S_["var1_ready"], 1)

            v.wait_ge(S_["ld_const"], 32)
            v.tensor_copy(repb[:, :], const("rep")[0:C, :]).then_inc(S_["repb_ready"], 1)
            v.tensor_copy(trib[:, :], const("tri")).then_inc(S_["repb_ready"], 1)
            v.tensor_copy(onesb[:, :], const("ones")).then_inc(S_["repb_ready"], 1)
            v.wait_ge(S_["ld_mask"], 16)
            ts(maskb[:, :], maskw[0:C, :], 0.0, MASKED, ALU.is_equal, ALU.mult).then_inc(S_["mask_ready"], 1)
            v.wait_ge(S_["mask_ready"], 1)
            v.wait_ge(S_["ld_w"], 16 * W_LOADS)
            hi, mid, lo = (bo_p[0:3, i * P:(i + 1) * P].bitcast(bf16) for i in range(3))
            f, r, acc3 = bo_f[0:3, :], bo_r[0:3, :], bo_s[0:3, :]
            third = const("third")
            steps = (lambda: v.tensor_copy(hi, f),
                     lambda: tt(r, f, hi, ALU.subtract),
                     lambda: v.tensor_copy(mid, r),
                     lambda: tt(r, r, mid, ALU.subtract),
                     lambda: v.tensor_copy(lo, r),
                     lambda: ts(acc3, hi, third[0:3, 0:1], None, ALU.mult),
                     lambda: v.scalar_tensor_tensor(acc3, mid, third[0:3, 1:2], acc3, ALU.mult, ALU.add),
                     lambda: v.scalar_tensor_tensor(acc3, lo, third[0:3, 2:3], acc3, ALU.mult, ALU.add),
                     lambda: v.tensor_copy(bo3[:, :], acc3))
            for i, one in enumerate(steps):
                one().then_inc(S_["bo_parts"], 1)
                v.wait_ge(S_["bo_parts"], i + 1)
            v.nop().then_inc(S_["wg_free"], 1)
            need(v, "k_ps", 0)
            for h in range(2):
                for sub in range(2):
                    last = ts(kbd[:, h, :, sub * C:(sub + 1) * C],
                              ps8[4 + h][:, 0:B * C].rearrange("p (b c) -> p b c", b=B),
                              bias_qk[:, 2 + h:3 + h], const("submask")[:, sub:sub + 1], ALU.add, ALU.mult)
                last.then_inc(S_["kbd_ready"], 1)
            for b in range(B):
                need(v, "v_ps", b)
                vm = const("vmask").rearrange("p (c j) -> p c j", c=NCH)
                tt(vbd[:, b, :, :, 0:DH].rearrange("p c j d -> p (c j) d"),
                   ps8[b][:, 0:NCH * 48].rearrange("p (c d) -> p c d", d=DH),
                   const("vmask").unsqueeze(2).broadcast_to([P, NCH * 3, DH]), ALU.mult)
                v.tensor_copy(vbd[:, b, :, :, DH], vm).then_inc(S_["vbd_ready"], 1)
            need(v, "gb_ps", 0)
            v.tensor_copy(gbias[:, :], bank[2][:, 0:E]).then_inc(S_["gb_ready"], 1)
            need(v, "rstd1_ready", 0)
            v.wait_ge(S_["mean1_ready"], 2)
            need(v, "gb_ready", 0)
            need(v, "probs_zero", 0)

            def norm1(t, m, s):
                freed(v, "xT_ps", t, 2)
                ts(xn[:, m % 2, :], store[:, bass.ds(t * D, D)], mean1[:, bass.ds(t, 1)], rstd1[:, bass.ds(t, 1)],
                   ALU.subtract, ALU.mult).then_inc(S_["xn"], 1)

            def softmax_shift(t, m, s):
                need(v, "scores", t)
                sc = sc_ps[:, :, 0:HCOLS].rearrange("p r (h c) -> p r h c", h=4)
                red(mx[:, :].rearrange("p (r h) -> p r h", r=4), sc, AX.X, ALU.max).then_inc(S_["score_max"], 1)
                need(v, "score_max", t)
                freed(v, "pT_ps2", t, 2)
                tt(probs[:, m % 2, 0:HC].rearrange("p (r h c) -> p r h c", r=4, h=4), sc,
                   mx[:, :].rearrange("p (r h) -> p r h", r=4).unsqueeze(3).broadcast_to([P, 4, 4, C]),
                   ALU.subtract).then_inc(S_["score_sub"], 1)

            def normalise(t, m, s):
                need(v, "pv", t)
                pvv = pv_ps.rearrange("p (h n) -> p h n", h=H)
                v.reciprocal(rsum[:, :], pvv[:, :, DH]).then_inc(S_["o_rcp"], 1)
                need(v, "o_rcp", t)
                freed(v, "oT_ps", t, 2)
                tt(o[:, m % 2, :].rearrange("p (h n) -> p h n", h=H), pvv[:, :, 0:DH],
                   rsum[:, :].unsqueeze(2).broadcast_to([P, H, DH]), ALU.mult).then_inc(S_["o"], 1)

            def residual(t, m, s):
                need(v, "y_ps", t)
                stored(v, x1_st, m, s)
                tt(x1[:, m % 2, :], y_ps, store[:, bass.ds(t * D, D)], ALU.add).then_inc(S_["x1"], 1)
                need(v, "x1", t)
                v.bn_stats(stats2[:, :], x1[:, m % 2, :]).then_inc(S_["stats2"], 1)
                need_apart(v, "stats2", t)
                v.bn_aggr(mv2[:, m % 2, :], stats2[:, :]).then_inc(S_["mv2"], 1)
                need(v, "mv2", t)
                freed(v, "rstd2", t, 2)
                ts(var2[:, m % 2:m % 2 + 1], mv2[:, m % 2, 1:2], EPS, None, ALU.add).then_inc(S_["var2"], 1)

            def norm2(t, m, s):
                need(v, "rstd2", t)
                stored(v, scat, m, s)
                ts(rowb[:, m, 0:D], x1[:, m % 2, :], mv2[:, m % 2, 0:1], rstd2[:, m % 2:m % 2 + 1],
                   ALU.subtract, ALU.mult).then_inc(S_["xn2"], 1)

            def route(t, m, s):
                iota = const("iota")
                need(v, "gate_exp", t)
                ts(gsum[:, :], gexp[:, m % 2, :], 1.0, None, ALU.add).then_inc(S_["gate_add"], 1)
                need(v, "gate_add", t)
                v.reciprocal(score[:, :], gsum[:, :]).then_inc(S_["score"], 1)
                need(v, "score", t)
                tt(sfc[:, :], score[:, :], gbias[:, :], ALU.add).then_inc(S_["sfc"], 1)
                need(v, "sfc", t)
                red(gmax[:, :], sfc[:, :].rearrange("p (g n) -> p g n", g=NG), AX.X, ALU.max).then_inc(S_["gmax"], 1)
                need_apart(v, "gmax", t)
                v.max(gtop[:, :], gmax[:, :]).then_inc(S_["gtop"], 1)
                need_apart(v, "gtop", t)
                v.max_index(gidx[:, :], gtop[:, :], gmax[:, :]).then_inc(S_["gidx"], 1)
                need(v, "gidx", t)
                tt(ghot[:, :, :], iota[:, 0:NG].unsqueeze(2).broadcast_to([P, NG, TOPG]),
                   gidx[:, 0:TOPG].unsqueeze(1).broadcast_to([P, NG, TOPG]), ALU.is_equal).then_inc(S_["ghot"], 1)
                need(v, "ghot", t)
                red(gsel[:, :], ghot[:, :, :], AX.X, ALU.add).then_inc(S_["gsel"], 1)
                need(v, "gsel", t)
                tt(masked[:, :].rearrange("p (g n) -> p g n", g=NG), sfc[:, :].rearrange("p (g n) -> p g n", g=NG),
                   gsel[:, :].unsqueeze(2).broadcast_to([P, NG, GS]), ALU.mult).then_inc(S_["masked"], 1)
                need_apart(v, "masked", t)
                v.max(etop[:, :], masked[:, :]).then_inc(S_["etop"], 1)
                need_apart(v, "etop", t)
                v.max_index(eidx[:, :], etop[:, :], masked[:, :]).then_inc(S_["eidx"], 1)
                need(v, "eidx", t)
                tt(ehot[:, :, :], iota.unsqueeze(2).broadcast_to([P, E, TOPK]),
                   eidx[:, 0:TOPK].unsqueeze(1).broadcast_to([P, E, TOPK]), ALU.is_equal).then_inc(S_["ehot"], 1)
                need(v, "ehot", t)
                red(sel[:, :], ehot[:, :, :], AX.X, ALU.max).then_inc(S_["sel"], 1)
                need(v, "sel", t)
                v.scalar_tensor_tensor(wsel[:, :], sel[:, :], 1.0, score[:, :], ALU.mult, ALU.mult,
                                       accum_out=wsum[:, 0:1]).then_inc(S_["wsel"], 1)
                need(v, "wsel", t)
                ts(wsum[:, 1:2], wsum[:, 0:1], 1e-20, None, ALU.add).then_inc(S_["wsum_e"], 1)
                need(v, "wsum_e", t)
                v.reciprocal(wsum[:, 2:3], wsum[:, 1:2]).then_inc(S_["wsum_r"], 1)
                need(v, "wsum_r", t)
                ts(rowb[:, m, D:D + E], wsel[:, :], wsum[:, 2:3], ROUTE_SCALE, ALU.mult,
                   ALU.mult).then_inc(S_["row_w"], 1)

            def places(t, m, s):
                need(v, "rank", t)
                tt(place[:, :], rk_ps, const("region"), ALU.add).then_inc(S_["place"], 1)
                tt(selcum[:, :], selcum[:, :], sel[:, :], ALU.add).then_inc(S_["selcum"], 1)
                need(v, "place", t)
                tt(placek[:, :, :], ehot[:, :, :].rearrange("p e k -> p k e"),
                   place[:, :].unsqueeze(1).broadcast_to([P, TOPK, E]), ALU.mult).then_inc(S_["placek"], 1)
                need(v, "placek", t)
                dest_free(v, m, s)
                with nc.allow_low_precision(reason="whole numbers below 2**24"):
                    red(dest[:, m % 2, 0:TOPK], placek[:, :, :], AX.X, ALU.add).then_inc(S_["dest"], 1)

            def step(tile):
                at_tile(tile, -1, norm1)
                at_tile(tile, 3, norm2)
                at_tile(tile, 5, places)
                at_tile(tile, 4, route)
                at_tile(tile, 0, softmax_shift)
                at_tile(tile, 1, normalise)
                at_tile(tile, 2, residual)
            over_tiles(v, step)

            need(v, "counts", 0)
            v.tensor_copy(cnt[:, :], rk_ps).then_inc(S_["cnt"], 1)
            need(v, "cnt", 0)
            tt(tails[0:1, :], cnt[0:1, :], const("region")[0:1, :], ALU.add).then_inc(S_["tail_rows"], 1)
            cmp = pTf[:, 0:E * E].rearrange("p (a b) -> p a b", a=E)
            ts(blkcum[:, :], const("iota"), float(P), None, ALU.mult).then_inc(S_["sch_a"], 1)
            v.wait_ge(S_["sch_a"], 1)
            tt(cmp, cnt[:, :].unsqueeze(2).broadcast_to([P, E, E]),
               blkcum[:, :].unsqueeze(1).broadcast_to([P, E, E]), ALU.is_gt).then_inc(S_["sch_a"], 1)
            v.wait_ge(S_["sch_a"], 2)
            red(blocks[:, :], cmp, AX.X, ALU.add).then_inc(S_["sch_a"], 1)
            v.wait_ge(S_["sch_a"], 3)
            tt(cmp, const("iota").unsqueeze(2).broadcast_to([P, E, E]),
               const("iota").unsqueeze(1).broadcast_to([P, E, E]), ALU.is_ge).then_inc(S_["sch_a"], 1)
            v.wait_ge(S_["sch_a"], 4)
            tt(cmp, cmp, blocks[:, :].unsqueeze(1).broadcast_to([P, E, E]), ALU.mult).then_inc(S_["sch_a"], 1)
            v.wait_ge(S_["sch_a"], 5)
            red(blkcum[:, :], cmp, AX.X, ALU.add).then_inc(S_["sch_b"], 1)
            v.wait_ge(S_["sch_b"], 1)
            le = cmp[:, 0:2, :]
            jt = const("jtile")
            tt(le, blkcum[:, :].unsqueeze(1).broadcast_to([P, 2, E]), jt.unsqueeze(2).broadcast_to([P, 2, E]),
               ALU.is_le).then_inc(S_["sch_c"], 1)
            v.wait_ge(S_["sch_c"], 1)
            red(sched[:, 0:2], le, AX.X, ALU.add).then_inc(S_["sch_c"], 1)
            tt(cmp[:, 2:4, :], le, blocks[:, :].unsqueeze(1).broadcast_to([P, 2, E]), ALU.mult).then_inc(S_["sch_c"], 1)
            v.wait_ge(S_["sch_c"], 3)
            red(sched[:, 2:4], cmp[:, 2:4, :], AX.X, ALU.add).then_inc(S_["sch_d"], 1)
            v.wait_ge(S_["sch_d"], 1)
            tt(sched[:, 2:4], jt, sched[:, 2:4], ALU.subtract).then_inc(S_["sch_d"], 1)
            v.wait_ge(S_["sch_d"], 2)
            ts(sched[:, 2:4], sched[:, 2:4], float(P), None, ALU.mult).then_inc(S_["sch_d"], 1)
            v.wait_ge(S_["sch_d"], 3)
            v.scalar_tensor_tensor(sched[:, 2:4], sched[:, 0:2], float(REGION), sched[:, 2:4], ALU.mult,
                                   ALU.add).then_inc(S_["sch_d"], 1)
            v.wait_ge(S_["sch_d"], 4)
            ts(sched2[:, 2:4], sched[:, 2:4], float(PAD_ROW), None, ALU.min)
            ts(sched2[:, 0:2], sched[:, 0:2], float(E - 1), None, ALU.min).then_inc(S_["sch_e"], 1)
            need(v, "sch_ps", 0)
            v.tensor_copy(table[:, :], bank[3][0:1, :]).then_inc(S_["table"], 1)
            need(v, "table", 0)

            def hidden(j, m, q):
                need(v, "act", j)
                freed(v, "hidT_ps", j, 2)
                tt(hid[:, m % 2, :], act[:, m % 2, :], ps8[2 + m % 2][:, I:2 * I], ALU.mult).then_inc(S_["hid"], 1)

            def ev_hidT(j, m, q):
                need(v, "hidT_ps", j)
                freed(v, "ye_ps", j, 2)
                v.tensor_copy(hidT[:, m % 2, :], ps8[4 + m % 2][:, 0:I]).then_inc(S_["hidT"], 1)

            def weigh(j, m, q):
                e = v.value_load(table[0:1, bass.ds(j, 1)], min_val=0, max_val=E - 1)
                need(v, "ye_ps", j)
                if not (isinstance(j, int) and j < R_ACC):
                    v.wait_ge(acc_add[m % R_ACC], (q * (UB // R_ACC) + m // R_ACC) * 16)
                ts(ye[:, m % R_ACC, :], ps8[6 + m % 2][:, 0:D], xe[:, m, bass.ds(e + D, 1)], None,
                   ALU.mult).then_inc(S_["ye"], 1)

            def estep(tile):
                at_tile(tile, 0, hidden)
                at_tile(tile, 1, ev_hidT)
                at_tile(tile, 2, weigh)
            over_expert_tiles(v, estep)

            def s_hidden(s):
                for h in range(2):
                    v.wait_ge(S_["shg"], 2 * s + h + 1)
                    if s >= 2:
                        need(v, "sy_ps", s - 2, B)
                    tt(shh[:, (s % 2) * 2 + h, :], shg[:, h, :], ps8[2 * h + 1], ALU.mult).then_inc(S_["shh"], 1)

            def s_sum(s):
                v.wait_ge(ld_acc[s % 2], 16 * R_ACC * (s // 2 + 1))
                a0 = acc_in[:, (s % 2) * R_ACC, :]
                for r in range(1, R_ACC):
                    tt(a0, a0, acc_in[:, (s % 2) * R_ACC + r, :], ALU.add).then_inc(S_["acc_sum"], 1)
                    v.wait_ge(S_["acc_sum"], s * (R_ACC - 1) + r)
                if s >= 2:
                    v.wait_ge(S_["out_st"], 16 * (s - 1))
                for b in range(B):
                    v.wait_ge(S_["sy_ps"], s * B + b + 1)
                    tt(outb[:, s % 2, b * D:(b + 1) * D], ps8[4 + b][:, 0:D], a0[:, b * D:(b + 1) * D],
                       ALU.add).then_inc(S_["outb"], 1)
            for s in range(SB + 1):
                if s < SB:
                    s_hidden(s)
                if s >= 1:
                    s_sum(s - 1)


def kernel(x, ctx_1024, mask_SxS2_ik0, L0_xattn_Wq, L0_xattn_bq, L0_xattn_Wk, L0_xattn_bk, L0_xattn_Wv, L0_xattn_bv,
           L0_xattn_Wo, L0_xattn_bo, L0_ffn_gate_weight, L0_ffn_e_score_correction_bias, L0_ffn_experts_gate_up,
           L0_ffn_experts_down, L0_ffn_shared_gate_w, L0_ffn_shared_up_w, L0_ffn_shared_down_w):
    import concourse.bacc as bacc
    from concourse.bass_utils import run_bass_kernel_spmd

    order = np.array([(4 * r + 2 * h + sub) * DH + d
                      for h in range(2) for r in range(4) for sub in range(2) for d in range(DH)])
    wq, wk = np.asarray(L0_xattn_Wq).T[:, order], np.asarray(L0_xattn_Wk).T[:, order]
    bq, bk = (np.asarray(b)[order].reshape(2, P).T for b in (L0_xattn_bq, L0_xattn_bk))
    const, ids = constants()
    arrays = {
        "x": x, "mask": np.asarray(mask_SxS2_ik0).T, "wq": wq, "wk": wk,
        "wv": np.asarray(L0_xattn_Wv).T, "wo": np.asarray(L0_xattn_Wo).T,
        "bqk": np.concatenate([bq, bk], 1), "bvo": np.stack([L0_xattn_bv, L0_xattn_bo]),
        "ctx_t": np.asarray(ctx_1024).transpose(0, 2, 1),
        "gate_w": np.asarray(L0_ffn_gate_weight).T, "gate_b": L0_ffn_e_score_correction_bias,
        "egu": np.asarray(L0_ffn_experts_gate_up).transpose(0, 2, 1),
        "edn": np.asarray(L0_ffn_experts_down).transpose(0, 2, 1),
        "sgu": np.concatenate([np.asarray(L0_ffn_shared_gate_w).T, np.asarray(L0_ffn_shared_up_w).T], 1),
        "sdn": np.asarray(L0_ffn_shared_down_w).T, "const": const, "ids": ids,
    }
    arrays = {f"in_{n}": np.ascontiguousarray(a) for n, a in arrays.items()}
    nc = bacc.Bacc("TRN2", target_bir_lowering=False, num_devices=1)
    aps = [nc.dram_tensor(n, a.shape, mybir.dt.from_np(a.dtype), kind="ExternalInput").ap() for n, a in arrays.items()]
    out = nc.dram_tensor("out", (B, S, D), mybir.dt.float32, kind="ExternalOutput").ap()
    build(nc, *aps, out)
    return run_bass_kernel_spmd(nc, [arrays], core_ids=[0]).results[0]["out"]
```

```python
import concourse.bass as bass
from concourse import mybir
from contextlib import ExitStack
import numpy as np

B, S, D = 4, 1024, 256
C, H, DH = 77, 16, 16
E, I, TOPK = 32, 128, 6
NG, GS, TOPG = 8, 4, 4
SI = 256
P = 128
KT = D // P
NT = B * S // P
SB = S // P
ROUTE_SCALE = 2.5
EPS = 1e-5
HC = H * C
NCH = -(-HC // P)
PV = DH + 1
HCOLS = 4 * C
MASKED = -float(2 ** 60)
ROW = D + E + 1
REGION = B * S + P
PAD_ROW = E * REGION
NTB = -(-((B * S * TOPK + E * (P - 1)) // P) // 16) * 16
R_ACC = 4
RX = 16
W_LOADS = 5 + 4 * KT + 3 + 3
NPR = NTB // 2
ATT = 7 * 2 * D + 3 * NCH * P + 4 * ROW
UA, UB = 4, RX // 2


def chunk_head(c):
    return min(P * c // C, H - 3)


CONST = {}


def _const_layout():
    at = 0
    for name, n in (("ident", P), ("submask", 2), ("vmask", NCH * 3), ("iota", E), ("region", E),
                    ("jtile", 2), ("third", 3), ("half_neg", E), ("tri", P), ("ones", P), ("rep", HCOLS)):
        CONST[name] = (at, at + n)
        at += n
    return at


NCONST = _const_layout()


def constants():
    c = np.zeros((P, NCONST), np.float32)

    def put(name, a):
        lo, hi = CONST[name]
        c[:, lo:hi] = a
    p = np.arange(P)[:, None]
    put("ident", np.eye(P))
    put("submask", (p % 32) // DH == np.arange(2)[None])
    vm = np.zeros((P, NCH, 3))
    for ch in range(NCH):
        row = ch * P + np.arange(P)
        for j in range(3):
            vm[:, ch, j] = (row // C == chunk_head(ch) + j) & (row < HC)
    put("vmask", vm.reshape(P, -1))
    put("iota", np.arange(E)[None])
    put("region", REGION * np.arange(E)[None])
    put("jtile", p + P * np.arange(2)[None])
    put("third", p == np.arange(3)[None])
    put("half_neg", -0.5)
    put("tri", p < np.arange(P)[None])
    put("ones", 1.0)
    put("rep", p == np.arange(HCOLS)[None] % C)
    ids = np.zeros((P, NT + 1), np.int32)
    t = np.arange(NT)[None]
    ids[:, :NT] = (t % B) * S + (t // B) * P + p
    ids[:, NT] = B * S + p[:, 0]
    return c, ids


def build(nc, x, mask, wq, wk, wv, wo, bqk, bvo, ctx_t, gate_w, gate_b, egu, edn, sgu, sdn, const_in, ids_in, out):
    fp32, bf16, i32, u32 = mybir.dt.float32, mybir.dt.bfloat16, mybir.dt.int32, mybir.dt.uint32
    ALU, ACT, AX = mybir.AluOpType, mybir.ActivationFunctionType, mybir.AxisListType

    rows = nc.dram_tensor("rows", (PAD_ROW + P, ROW), fp32, kind="Internal").ap()
    acc = [nc.dram_tensor(f"acc{r}", (REGION, D), fp32, kind="Internal").ap() for r in range(R_ACC)]

    with ExitStack() as ctx:
        def sb(name, shape, dt=fp32):
            return ctx.enter_context(nc.sbuf_tensor(name, shape, dt))

        S_ = {}

        def sem(name):
            S_[name] = ctx.enter_context(nc.semaphore(name))
            return S_[name]

        wgu = sb("wgu", [P, E * KT * 2 * I])
        wdn = sb("wdn", [P, E * D])
        wsgu = sb("wsgu", [P, KT, 2 * SI])
        wsdn = sb("wsdn", [P, KT, D])
        wq_sb = sb("wq_sb", [P, KT, D])
        wo_sb = sb("wo_sb", [P, KT, D])
        wg_sb = sb("wg_sb", [P, KT, E])
        kbd = sb("kbd", [P, 2, B, 2 * C])
        vbd = sb("vbd", [P, B, NCH, 3, PV])
        maskb = sb("maskb", [C, S], bf16)
        repb = sb("repb", [C, HCOLS], bf16)
        trib = sb("trib", [P, P], bf16)
        onesb = sb("onesb", [P, P], bf16)
        cst = sb("cst", [P, NCONST])
        ids = sb("ids", [P, NT + 1], i32)
        bias_qk = sb("bias_qk", [P, 4])
        bo3 = sb("bo3", [3, D], bf16)
        gbias = sb("gbias", [P, E])
        store = sb("store", [P, NT * D])
        stats1 = sb("stats1", [P, NT, 6])
        mean1 = sb("mean1", [P, NT])
        shift1 = sb("shift1", [P, NT])
        rstd1 = sb("rstd1", [P, NT])
        tmp1 = sb("tmp1", [P, 2, NT])
        work = sb("work", [P, ATT])
        mx = sb("mx", [P, H])
        rsum = sb("rsum", [P, H])
        stats2 = sb("stats2", [P, 6])
        mv2 = sb("mv2", [P, 2, 2])
        var2 = sb("var2", [P, 2])
        rstd2 = sb("rstd2", [P, 2])
        gexp = sb("gexp", [P, 2, E])
        gsum = sb("gsum", [P, E])
        score = sb("score", [P, E])
        sfc = sb("sfc", [P, E])
        gmax = sb("gmax", [P, NG])
        gtop = sb("gtop", [P, 8])
        gidx = sb("gidx", [P, 8], u32)
        ghot = sb("ghot", [P, NG, TOPG])
        gsel = sb("gsel", [P, NG])
        masked = sb("masked", [P, E])
        etop = sb("etop", [P, 8])
        eidx = sb("eidx", [P, 8], u32)
        ehot = sb("ehot", [P, E, TOPK])
        sel = sb("sel", [P, E], bf16)
        selcum = sb("selcum", [P, E], bf16)
        wsel = sb("wsel", [P, E])
        wsum = sb("wsum", [P, 4])
        place = sb("place", [P, E])
        placek = sb("placek", [P, TOPK, E])
        dest = sb("dest", [P, 2, 8], u32)
        padrow = sb("padrow", [P, ROW])
        cnt = sb("cnt", [P, E])
        blocks = sb("blocks", [P, E])
        blkcum = sb("blkcum", [P, E])
        sched = sb("sched", [P, 4])
        sched2 = sb("sched2", [P, 4])
        table = sb("table", [1, 4 * P], i32)
        tails = sb("tails", [1, E], i32)

        att = []

        def carve(base, at, shape):
            n = int(np.prod(shape[1:]))
            v = base[:, at:at + n]
            names = "abcd"[:len(shape) - 1]
            if len(shape) > 2:
                v = v.rearrange("p (%s) -> p %s" % (" ".join(names), " ".join(names)),
                                **{k: d for k, d in zip(names[1:], shape[2:])})
            return v, at + n
        wk_sb, at = carve(wdn, 0, [P, KT, D])
        wv_sb, at = carve(wdn, at, [P, KT, D])
        ctxT, at = carve(wdn, at, [P, KT, B * C])
        ctx3, at = carve(wdn, at, [P, KT, B, 3 * C])
        bv_row, at = carve(wdn, at, [P, D])
        gb_row, at = carve(wdn, at, [P, E])
        bo_f, at = carve(wdn, at, [P, D])
        bo_r, at = carve(wdn, at, [P, D])
        bo_s, at = carve(wdn, at, [P, D])
        assert at <= E * D
        maskw = wgu[:, 0:S].bitcast(i32)
        bo_p = wgu[:, S:S + 3 * P]

        at = 0
        for shape in ([P, 2, D],) * 7 + ([P, 2, NCH * P], [P, NCH, P], [P, 4, ROW]):
            v_, at = carve(work, at, shape)
            att.append(v_)
        assert at == ATT
        xn, xnT, qT, o, oT, x1, xn2T, probs, pT, rowb = att
        pTf = pT.rearrange("p a b -> p (a b)")
        xe, at = carve(work, 0, [P, RX, ROW])
        xeT, at = carve(work, at, [P, 2, 2 * D])
        act, at = carve(work, at, [P, 2, 2 * I])
        hid, at = carve(work, at, [P, 2, 2 * I])
        hidT, at = carve(work, at, [P, 2, 2 * I])
        ye, at = carve(work, at, [P, R_ACC, D])
        assert at <= ATT
        acc_in, at = carve(wgu, 0, [P, 2 * R_ACC, B * D])
        shg, at = carve(wgu, at, [P, 2, B * P])
        shh, at = carve(wgu, at, [P, 4, B * P])
        outb, at = carve(wgu, at, [P, 2, B * D])
        assert at <= E * KT * 2 * I

        bank = [ctx.enter_context(nc.psum_tensor(f"bank{i}", [P, 512], fp32)) for i in range(4, 8)]
        sc_ps = ctx.enter_context(nc.psum_tensor("sc_ps", [P, 4, 512], fp32))
        xT_ps = bank[0][:, 0:D].rearrange("p (k n) -> p k n", k=KT)
        pT_ps = [bank[1], bank[2], bank[1]]
        oT_ps = bank[3][:, 0:D]
        x2T_ps = xT_ps
        q_ps = bank[2][:, 0:D]
        pv_ps = bank[3][:, 0:H * PV]
        y_ps = bank[0][:, 0:D]
        lg_ps = bank[1][:, 0:E]
        rk_ps = bank[2][:, 0:E]
        ps8 = [sc_ps[:, i, :] for i in range(4)] + [b[:, :] for b in bank]

        for name in ("ld_const ld_w ld_gate ld_egu ld_edn ld_mask cst_b k_ps kbd_ready v_ps vbd_ready gb_ps gb_ready "
                     "bo_parts mask_ready repb_ready pad_ready pool_go probs_zero setup_read wg_free stats1_ready "
                     "mean1_ready norm1_ready tmp_ready var1_ready "
                     "rstd1_ready sel_zero acc_init pad_init "
                     "xn xT_ps xnT q_ps qT scores score_max0 score_max1 score_sub probs pT_ps0 pT_ps1 pT_ps2 pT0 pT1 pT2 pv o_rcp o "
                     "oT_ps oT y_ps x1 stats2 mv2 var2 rstd2 row_id xn2 x2T_ps xn2T logits gate_exp "
                     "gate_add score sfc gmax gtop gidx ghot gsel masked etop eidx ehot sel wsel wsum_e wsum_r row_w "
                     "rank place placek dest selcum "
                     "counts cnt sch_a sch_b sch_c sch_d sch_e sch_ps table tail_rows "
                     "xeT_ps xeT gu_ps act hid hidT_ps hidT ye_ps ye "
                     "sg_ps shg shh sy_ps acc_sum outb out_st").split():
            sem(name)
        ld_x = [sem(f"ld_x{i}") for i in range(SB)]
        x1_st = [sem(f"x1_st{i}") for i in range(2)]
        xn2T_st = [sem(f"xn2T_st{i}") for i in range(2)]
        scat = [sem(f"scat{i}") for i in range(4)]
        tails_st = [sem(f"tails_st{i}") for i in range(3)]
        ld_xe = [sem(f"ld_xe{i}") for i in range(RX)]
        acc_add = [sem(f"acc_add{i}") for i in range(R_ACC)]
        ld_acc = [sem(f"ld_acc{i}") for i in range(2)]

        def need(eng, name, t, per=1):
            eng.wait_ge(S_[name], (t + 1) * per)

        def need_apart(eng, name, t):
            eng.wait_ge(S_[name], 1)
            need(eng, name, t)

        def freed(eng, name, t, ring, per=1):
            if isinstance(t, int) and t < ring:
                return
            eng.wait_ge(S_[name], (t - (ring - 1)) * per)

        def stored(eng, sems, m, s):
            n = len(sems)
            per = 16 * TOPK if n == 4 else 16
            count = s * (UA // n) + m // n
            if not (isinstance(count, int) and count == 0):
                eng.wait_ge(sems[m % n], count * per)

        def dest_free(eng, m, s):
            count = s + 1 if m >= 2 else s
            if not (isinstance(count, int) and count == 0):
                eng.wait_ge(scat[(m + 2) % 4], count * 16 * TOPK)

        def read_out(eng, name, t, ahead):
            n = t + ahead + 1
            if not isinstance(n, int):
                eng.wait_ge(S_[name], n)
            elif n > 0:
                eng.wait_ge(S_[name], min(n, NT))

        def const(name):
            lo, hi = CONST[name]
            return cst[:, lo:hi]

        block = ctx.enter_context(nc.Block())

        TAILS = [0, 11, 22, E]

        def store_tails(eng, q):
            need(eng, "tail_rows", 0)
            with eng.Fori(TAILS[q], TAILS[q + 1]) as e:
                r = eng.value_load(tails[0:1, bass.ds(e, 1)], min_val=0, max_val=PAD_ROW - P)
                eng.dma_start(rows[bass.ds(r, P), :], padrow[:, :]).then_inc(tails_st[q], 16)

        LEAD, LAG = 1, 5
        FIRST, TRIPS = 7, (NT - LEAD - 7) // UA
        LAST = FIRST + UA * TRIPS

        def over_tiles(eng, step):
            def fixed(n):
                def tile(lag):
                    t = n - lag
                    return (t, t % UA, t // B) if 0 <= t < NT else None
                return tile
            for n in range(-LEAD, FIRST):
                step(fixed(n))
            with eng.Fori(0, TRIPS) as k:
                for u in range(UA):
                    def tile(lag, u=u):
                        base = FIRST + u - lag
                        return (k * UA + base, base % UA, k + base // B)
                    step(tile)
            for n in range(LAST, NT + LAG):
                step(fixed(n))

        def at_tile(tile, lag, stage):
            got = tile(lag)
            if got is not None:
                stage(*got)

        BFIRST, BTRIPS = UB - 1, (NPR - UB) // UB
        BLAST = BFIRST + UB * BTRIPS

        def over_pairs(eng, step):
            def fixed(n):
                def tile(lag):
                    i = n - lag
                    return (i, i % UB, i // UB) if 0 <= i < NPR else None
                return tile
            for n in range(-1, BFIRST):
                step(fixed(n))
            with eng.Fori(0, BTRIPS) as k:
                for u in range(UB):
                    def tile(lag, u=u):
                        base = BFIRST + u - lag
                        return (k * UB + base, base % UB, k + base // UB)
                    step(tile)
            for n in range(BLAST, NPR + 2):
                step(fixed(n))

        @block.sync
        def _(sp):
            sp.dma_start(cst[:, :], const_in[:, :]).then_inc(S_["ld_const"], 16)
            for k in range(KT):
                sp.dma_start(ctxT[:, k, :].rearrange("p (b c) -> p b c", b=B),
                             ctx_t[:, k * P:(k + 1) * P, :].rearrange("b p c -> p b c")).then_inc(S_["ld_w"], 16)
                for i in range(3):
                    sp.dma_start(ctx3[:, k, :, i * C:(i + 1) * C],
                                 ctx_t[:, k * P:(k + 1) * P, :].rearrange("b p c -> p b c")).then_inc(S_["ld_w"], 16)
            sp.dma_start(maskw[0:C, :], mask).then_inc(S_["ld_mask"], 16)
            for s in range(SB):
                sp.dma_start(store[:, s * B * D:(s + 1) * B * D].rearrange("p (b d) -> p b d", b=B),
                             x[:, s * P:(s + 1) * P, :].rearrange("b p d -> p b d")).then_inc(ld_x[s], 16)
            need(sp, "wg_free", 0)
            for e0 in range(0, E, 8):
                sp.dma_start(wgu[:, e0 * 512:(e0 + 8) * 512].rearrange("p (e k n) -> p e k n", e=8, k=KT),
                             egu[e0:e0 + 8].rearrange("e (k p) n -> p e k n", p=P)).then_inc(S_["ld_egu"], 16)
            need(sp, "pad_ready", 0)
            for r in range(R_ACC):
                n0 = B * S if r == 0 else 0
                n = (REGION - n0) // P
                sp.dma_start(acc[r][n0:REGION, :].rearrange("(n p) d -> p n d", p=P),
                             padrow[:, 0:D].unsqueeze(1).broadcast_to([P, n, D])).then_inc(S_["acc_init"], 16)
            sp.dma_start(rows[PAD_ROW:PAD_ROW + P, :], padrow[:, :]).then_inc(tails_st[0], 16)
            sp.dma_start(wsgu[:, :, :], sgu.rearrange("(k p) n -> p k n", p=P)).then_inc(S_["ld_egu"], 16)
            sp.dma_start(wsdn[:, :, :], sdn.rearrange("(k p) n -> p k n", p=P)).then_inc(S_["ld_egu"], 16)
            sp.wait_ge(S_["kbd_ready"], 2)
            need(sp, "vbd_ready", 0, B)
            need(sp, "gb_ready", 0)
            sp.wait_ge(S_["bo_parts"], 9)
            for e0 in range(0, E, 8):
                sp.dma_start(wdn[:, e0 * D:(e0 + 8) * D].rearrange("p (e n) -> p e n", e=8),
                             edn[e0:e0 + 8].rearrange("e p n -> p e n")).then_inc(S_["ld_edn"], 16)

            def st_x1(t, m, s):
                need(sp, "x1", t)
                sp.dma_start(acc[0][bass.ds(s * P + (m * S), P), :], x1[:, m % 2, :]).then_inc(x1_st[m % 2], 16)

            def st_xn2T(t, m, s):
                need(sp, "xn2T", t)
                sp.dma_start(store[:, bass.ds(t * D, D)], xn2T[:, m % 2, :]).then_inc(xn2T_st[m % 2], 16)

            def step(tile):
                at_tile(tile, 3, st_x1)
                at_tile(tile, 3, st_xn2T)
            over_tiles(sp, step)

            store_tails(sp, 0)
            need(sp, "table", 0)
            for q in range(3):
                sp.wait_ge(tails_st[q], 16 * (TAILS[q + 1] - TAILS[q] + (q == 0)))
            for one in scat:
                sp.wait_ge(one, 16 * TOPK * NT // 4)

            def ld_tile(j, m):
                r = sp.value_load(table[0:1, bass.ds(j + 2 * P, 1)], min_val=0, max_val=PAD_ROW)
                sp.dma_start(xe[:, m, :], rows[bass.ds(r, P), :]).then_inc(ld_xe[m], 16)
            for j in range(RX):
                ld_tile(j, j)
            with sp.Fori(1, NTB // RX) as k:
                for u in range(RX):
                    sp.wait_ge(acc_add[u % R_ACC], ((k - 1) * (RX // R_ACC) + u // R_ACC + 1) * 16)
                    ld_tile(k * RX + u, u)

            for r in range(R_ACC):
                sp.wait_ge(acc_add[r], 16 * (NTB // R_ACC))
            need(sp, "gu_ps", NPR - 1)

            def ld_accs(s, m):
                for r in range(R_ACC):
                    sp.dma_start(acc_in[:, m * R_ACC + r, :].rearrange("p (b d) -> p b d", b=B),
                                 acc[r][0:B * S, :].rearrange("(b q) d -> q b d", b=B)[bass.ds(s * P, P), :, :]
                                 ).then_inc(ld_acc[m], 16)

            def st_out(s, m):
                need(sp, "outb", s, B)
                sp.dma_start(out.rearrange("b q d -> q b d")[bass.ds(s * P, P), :, :],
                             outb[:, m, :].rearrange("p (b d) -> p b d", b=B)).then_inc(S_["out_st"], 16)
            ld_accs(0, 0)
            ld_accs(1, 1)
            for s in range(SB):
                st_out(s, s % 2)
                if s + 2 < SB:
                    need(sp, "acc_sum", s, R_ACC - 1)
                    ld_accs(s + 2, s % 2)
            sp.wait_ge(S_["out_st"], 16 * SB)

        @block.gpsimd
        def _(pool):
            pool.memset(padrow[:, :], 0.0).then_inc(S_["pad_init"], 1)
            pool.memset(probs[:, :, HC:NCH * P], 0.0).then_inc(S_["probs_zero"], 1)
            pool.memset(selcum[:, :], 0.0).then_inc(S_["selcum"], 1)
            pool.wait_ge(S_["ld_const"], 32)
            pool.wait_ge(S_["pad_init"], 1)
            pool.tensor_copy(padrow[:, ROW - 1:ROW].bitcast(i32), ids[:, NT:NT + 1]).then_inc(S_["pad_ready"], 1)
            need(pool, "var1_ready", 0)
            pool.tensor_tensor(rstd1[:, :], tmp1[:, 0, :], const("half_neg"), ALU.pow).then_inc(S_["rstd1_ready"], 1)

            def scatter(t, m, s):
                need(pool, "dest", t)
                need(pool, "row_id", t)
                pool.sem_inc(S_["pool_go"], 1)
                pool.wait_ge(S_["pool_go"], 1)
                for k in range(TOPK):
                    pool.indirect_dma_start(rows[:, :], bass.IndirectOffsetOnAxis(ap=dest[:, m % 2, k:k + 1], axis=0),
                                            rowb[:, m, :], None).then_inc(scat[m], 16)

            def ids_and_rstd2(t, m, s):
                stored(pool, scat, m, s)
                pool.tensor_copy(rowb[:, m, ROW - 1:ROW].bitcast(i32), ids[:, bass.ds(t, 1)]).then_inc(S_["row_id"], 1)
                need(pool, "var2", t)
                freed(pool, "xn2", t, 2)
                pool.tensor_tensor(rstd2[:, m % 2:m % 2 + 1], var2[:, m % 2:m % 2 + 1], const("half_neg")[:, 0:1],
                                   ALU.pow).then_inc(S_["rstd2"], 1)

            def step(tile):
                at_tile(tile, 3, ids_and_rstd2)
                at_tile(tile, 5, scatter)
            over_tiles(pool, step)

            store_tails(pool, 2)
            pool.wait_ge(S_["acc_init"], 16 * R_ACC)
            for one in x1_st:
                pool.wait_ge(one, 16 * NT // 2)

            def add_rows(m):
                pool.indirect_dma_start(acc[m % R_ACC][:, :],
                                        bass.IndirectOffsetOnAxis(ap=xe[:, m, ROW - 1:ROW].bitcast(u32), axis=0),
                                        ye[:, m % R_ACC, :], None, compute_op=ALU.add).then_inc(acc_add[m % R_ACC], 16)
            for j in range(RX):
                need(pool, "ye", j)
                if j >= R_ACC:
                    pool.wait_ge(acc_add[j % R_ACC], 16 * (j // R_ACC))
                add_rows(j)
            with pool.Fori(1, NTB // RX) as k:
                for u in range(RX):
                    need(pool, "ye", k * RX + u)
                    pool.wait_ge(acc_add[u % R_ACC], (k * (RX // R_ACC) + u // R_ACC) * 16)
                    pool.sem_inc(S_["pool_go"], 1)
                    pool.wait_ge(S_["pool_go"], 1)
                    add_rows(u)

        @block.scalar
        def _(a):
            a.dma_start(ids[:, :], ids_in[:, :]).then_inc(S_["ld_const"], 16)
            for dst, src in ((wk_sb, wk), (wv_sb, wv), (wq_sb, wq), (wo_sb, wo), (wg_sb, gate_w)):
                a.dma_start(dst[:, :, :], src.rearrange("(k p) n -> p k n", p=P)).then_inc(S_["ld_w"], 16)
            for i in range(3):
                a.dma_start(bo_f[i:i + 1, :], bvo[1:2, :]).then_inc(S_["ld_w"], 16)
            a.dma_start(bias_qk[:, :], bqk).then_inc(S_["ld_w"], 16)
            a.dma_start(bv_row[0:1, :], bvo[0:1, :]).then_inc(S_["ld_w"], 16)
            a.dma_start(gb_row[0:1, :], gate_b.rearrange("(a n) -> a n", a=1)).then_inc(S_["ld_w"], 16)

            need(a, "norm1_ready", 0)

            def norm1(t, m, s):
                freed(a, "xT_ps", t, 2)
                a.activation(xn[:, m % 2, :], store[:, bass.ds(t * D, D)], ACT.Identity, bias=shift1[:, bass.ds(t, 1)],
                             scale=rstd1[:, bass.ds(t, 1)]).then_inc(S_["xn"], 1)

            def ev_xT(t, m, s):
                need(a, "xT_ps", t)
                freed(a, "q_ps", t, 2)
                a.activation(xnT[:, m % 2, :].rearrange("p (k n) -> p k n", k=KT), xT_ps, ACT.Copy).then_inc(S_["xnT"], 1)

            def ev_q(t, m, s):
                need(a, "q_ps", t)
                freed(a, "scores", t, 2)
                for h in range(2):
                    last = a.activation(qT[:, m % 2, h * P:(h + 1) * P], q_ps[:, h * P:(h + 1) * P], ACT.Identity,
                                        bias=bias_qk[:, h:h + 1])
                last.then_inc(S_["qT"], 1)

            def exps(t, m, s):
                need(a, "score_sub", t)
                a.activation(probs[:, m % 2, 0:HC], probs[:, m % 2, 0:HC], ACT.Exp,
                             scale=float(DH) ** -0.5).then_inc(S_["probs"], 1)

            def ev_pT(f):
                def stage(t, m, s):
                    need(a, f"pT_ps{f}", t)
                    if f == 0:
                        freed(a, "pv", t, 1)
                    n = min(4, NCH - 4 * f)
                    a.activation(pTf[:, 4 * f * P:(4 * f + n) * P], pT_ps[f][:, 0:n * P], ACT.Copy).then_inc(S_[f"pT{f}"], 1)
                return stage

            def ev_oT(t, m, s):
                need(a, "oT_ps", t)
                freed(a, "y_ps", t, 2)
                a.activation(oT[:, m % 2, :], oT_ps, ACT.Copy).then_inc(S_["oT"], 1)

            def ev_x2T(t, m, s):
                need(a, "x2T_ps", t)
                freed(a, "logits", t, 2)
                stored(a, xn2T_st, m, s)
                a.activation(xn2T[:, m % 2, :].rearrange("p (k n) -> p k n", k=KT), x2T_ps, ACT.Copy).then_inc(S_["xn2T"], 1)

            def gate_exp(t, m, s):
                need(a, "logits", t)
                freed(a, "gate_add", t, 2)
                a.activation(gexp[:, m % 2, :], lg_ps, ACT.Exp, scale=-1.0).then_inc(S_["gate_exp"], 1)

            def step(tile):
                at_tile(tile, -1, norm1)
                at_tile(tile, -1, ev_xT)
                at_tile(tile, 1, ev_pT(0))
                at_tile(tile, 1, ev_pT(1))
                at_tile(tile, 2, ev_oT)
                at_tile(tile, 3, ev_x2T)
                at_tile(tile, 1, ev_pT(2))
                at_tile(tile, -1, ev_q)
                at_tile(tile, 3, gate_exp)
                at_tile(tile, 0, exps)
            over_tiles(a, step)
            store_tails(a, 1)

            def ev_xeT(i, m, q):
                need(a, "xeT_ps", i)
                freed(a, "gu_ps", i, 2)
                a.activation(xeT[:, m % 2, :], ps8[m % 2], ACT.Copy).then_inc(S_["xeT"], 1)

            def silu(i, m, q):
                need(a, "gu_ps", i)
                freed(a, "hid", i, 2)
                a.activation(act[:, m % 2, :].rearrange("p (w n) -> p w n", w=2),
                             ps8[2 + m % 2].rearrange("p (w n) -> p w n", w=2)[:, :, 0:I], ACT.Silu).then_inc(S_["act"], 1)

            def pstep(tile):
                at_tile(tile, -1, ev_xeT)
                at_tile(tile, 0, silu)
            over_pairs(a, pstep)

            for s in range(SB):
                for h in range(2):
                    a.wait_ge(S_["sg_ps"], 2 * s + h + 1)
                    if s >= 1:
                        a.wait_ge(S_["shh"], 2 * (s - 1) + h + 1)
                    elif h == 0:
                        need(a, "gu_ps", NPR - 1)
                    a.activation(shg[:, h, :], ps8[2 * h], ACT.Silu).then_inc(S_["shg"], 1)

        @block.tensor
        def _(pe):
            mm = nc.tensor.matmul
            ident = const("ident")

            pe.wait_ge(S_["ld_const"], 32)
            pe.wait_ge(S_["ld_w"], 16 * W_LOADS)
            for h in range(2):
                for k in range(KT):
                    last = mm(ps8[4 + h][:, 0:B * C], wk_sb[:, k, h * P:(h + 1) * P], ctxT[:, k, :],
                              start=k == 0, stop=k == KT - 1)
            last.then_inc(S_["k_ps"], 1)
            ones_row = const("ones")[0:1, :]
            for b in range(B):
                for c in range(NCH):
                    off, n0 = c * P % C, chunk_head(c) * DH
                    cols = ps8[b][:, c * 48:c * 48 + 48]
                    for k in range(KT):
                        mm(cols, ctx3[:, k, b, off:off + P], wv_sb[:, k, n0:n0 + 48], start=k == 0, stop=False)
                    last = mm(cols, ones_row, bv_row[0:1, n0:n0 + 48], start=False, stop=True)
                last.then_inc(S_["v_ps"], 1)
            mm(bank[2][:, 0:E], ones_row, gb_row[0:1, :], start=True, stop=True).then_inc(S_["gb_ps"], 1)
            need(pe, "mask_ready", 0)
            need(pe, "repb_ready", 0, 3)
            need(pe, "gb_ready", 0)
            pe.wait_ge(S_["kbd_ready"], 2)
            pe.wait_ge(S_["vbd_ready"], B)
            pe.wait_ge(S_["bo_parts"], 9)
            need(pe, "probs_zero", 0)

            def tr_x(t, m, s):
                need(pe, "xn", t)
                read_out(pe, "x1", t, -4)
                if isinstance(t, int):
                    read_out(pe, "xnT", t, -1)
                for k in range(KT):
                    last = nc.tensor.transpose(xT_ps[:, k, :], xn[:, m % 2, k * P:(k + 1) * P], ident)
                last.then_inc(S_["xT_ps"], 1)

            def q_proj(t, m, s):
                need(pe, "xnT", t)
                read_out(pe, "pT1", t, -2)
                if isinstance(t, int):
                    read_out(pe, "qT", t, -1)
                for h in range(2):
                    for k in range(KT):
                        last = mm(q_ps[:, h * P:(h + 1) * P], wq_sb[:, k, h * P:(h + 1) * P],
                                  xnT[:, m % 2, k * P:(k + 1) * P], start=k == 0, stop=k == KT - 1)
                last.then_inc(S_["q_ps"], 1)

            def qk(t, m, s):
                need(pe, "qT", t)
                freed(pe, "score_sub", t, 1)
                for r in range(4):
                    mm(sc_ps[:, r, 0:HCOLS], maskb[:, bass.ds(s * P, P)], repb[:, :], start=True, stop=False,
                       skip_group_check=True)
                for h in range(2):
                    for r in range(4):
                        last = mm(sc_ps[:, r, h * 2 * C:(h + 1) * 2 * C],
                                  qT[32 * r:32 * r + 32, m % 2, h * P:(h + 1) * P],
                                  kbd[32 * r:32 * r + 32, h, m, :], start=False, stop=True, skip_group_check=True)
                last.then_inc(S_["scores"], 1)

            def tr_p(f):
                def stage(t, m, s):
                    if f == 0:
                        need(pe, "probs", t)
                        read_out(pe, "gate_exp", t, -3)
                        if isinstance(t, int):
                            read_out(pe, "pT2", t, -1)
                    if f == 1:
                        read_out(pe, "place", t, -4)
                        if isinstance(t, int):
                            read_out(pe, "qT", t, 1)
                            read_out(pe, "pT1", t, -1)
                    if f == 2:
                        read_out(pe, "pT0", t, 0)
                    for c in range(4 * f, min(4 * f + 4, NCH)):
                        last = nc.tensor.transpose(pT_ps[f][:, (c % 4) * P:(c % 4 + 1) * P],
                                                   probs[:, m % 2, c * P:(c + 1) * P], ident)
                    last.then_inc(S_[f"pT_ps{f}"], 1)
                return stage

            def pv(t, m, s):
                read_out(pe, "oT", t, -1)
                for c in range(NCH):
                    if c % 4 == 0:
                        need(pe, f"pT{c // 4}", t)
                    n0 = chunk_head(c) * PV
                    last = mm(pv_ps[:, n0:n0 + 3 * PV], pT[:, c, :], vbd[:, m, c, :, :].rearrange("p a b -> p (a b)"),
                              start=c == 0, stop=c == NCH - 1, skip_group_check=True)
                last.then_inc(S_["pv"], 1)

            def tr_o(t, m, s):
                need(pe, "o", t)
                for k in range(KT):
                    last = nc.tensor.transpose(oT_ps[:, k * P:(k + 1) * P], o[:, m % 2, k * P:(k + 1) * P], ident)
                last.then_inc(S_["oT_ps"], 1)

            def o_proj(t, m, s):
                need(pe, "oT", t)
                read_out(pe, "xn2T", t, -1)
                if isinstance(t, int):
                    read_out(pe, "xnT", t, 3)
                for k in range(KT):
                    mm(y_ps, oT[:, m % 2, k * P:(k + 1) * P], wo_sb[:, k, :], start=k == 0, stop=False)
                mm(y_ps, onesb[0:3, :], bo3[:, :], start=False, stop=True).then_inc(S_["y_ps"], 1)

            def tr_x2(t, m, s):
                need(pe, "xn2", t)
                read_out(pe, "xnT", t, 4)
                for k in range(KT):
                    last = nc.tensor.transpose(x2T_ps[:, k, :], rowb[:, m, k * P:(k + 1) * P], ident)
                last.then_inc(S_["x2T_ps"], 1)

            def gate(t, m, s):
                need(pe, "xn2T", t)
                read_out(pe, "pT2", t, 2)
                if isinstance(t, int):
                    read_out(pe, "gate_exp", t, -1)
                for k in range(KT):
                    last = mm(lg_ps, xn2T[:, m % 2, k * P:(k + 1) * P], wg_sb[:, k, :], start=k == 0, stop=k == KT - 1)
                last.then_inc(S_["logits"], 1)

            def rank(t, m, s):
                need(pe, "sel", t)
                need(pe, "selcum", t)
                read_out(pe, "qT", t, 5)
                if isinstance(t, int):
                    read_out(pe, "pT1", t, 3)
                    read_out(pe, "place", t, -1)
                mm(rk_ps, trib[:, :], sel[:, :], start=True, stop=False)
                mm(rk_ps, onesb[:, :], selcum[:, :], start=False, stop=True).then_inc(S_["rank"], 1)

            def step(tile):
                at_tile(tile, 0, qk)
                at_tile(tile, -1, tr_x)
                at_tile(tile, 1, tr_p(0))
                at_tile(tile, 1, tr_p(1))
                at_tile(tile, 2, tr_o)
                at_tile(tile, 3, tr_x2)
                at_tile(tile, 1, tr_p(2))
                at_tile(tile, -1, q_proj)
                at_tile(tile, 1, pv)
                at_tile(tile, 2, o_proj)
                at_tile(tile, 3, gate)
                at_tile(tile, 4, rank)
            over_tiles(pe, step)

            need(pe, "selcum", NT)
            mm(rk_ps, onesb[:, :], selcum[:, :], start=True, stop=True).then_inc(S_["counts"], 1)
            need(pe, "sch_e", 0)
            for i in range(4):
                last = mm(bank[3][0:1, i * P:(i + 1) * P], sched2[:, i:i + 1], ident, start=True, stop=True)
            last.then_inc(S_["sch_ps"], 1)
            need(pe, "table", 0)
            pe.wait_ge(S_["ld_egu"], 16 * 6)
            pe.wait_ge(S_["ld_edn"], 16 * 4)

            def tr_xe(i, m, q):
                for w in range(2):
                    pe.wait_ge(ld_xe[2 * m + w], (q + 1) * 16)
                    for k in range(KT):
                        last = nc.tensor.transpose(ps8[m % 2][:, (2 * w + k) * P:(2 * w + k + 1) * P],
                                                   xe[:, 2 * m + w, k * P:(k + 1) * P], ident)
                last.then_inc(S_["xeT_ps"], 1)

            def gate_up(i, m, q):
                for w in range(2):
                    e = pe.value_load(table[0:1, bass.ds(i * 2 + w, 1)], min_val=0, max_val=E - 1)
                    if w == 0:
                        need(pe, "xeT", i)
                    for k in range(KT):
                        last = mm(ps8[2 + m % 2][:, w * 2 * I:(w + 1) * 2 * I],
                                  xeT[:, m % 2, (2 * w + k) * P:(2 * w + k + 1) * P],
                                  wgu[:, bass.ds(e * 512 + k * 256, 256)], start=k == 0, stop=k == KT - 1)
                last.then_inc(S_["gu_ps"], 1)

            def tr_hid(i, m, q):
                need(pe, "hid", i)
                for w in range(2):
                    last = nc.tensor.transpose(ps8[4 + m % 2][:, w * I:(w + 1) * I], hid[:, m % 2, w * I:(w + 1) * I], ident)
                last.then_inc(S_["hidT_ps"], 1)

            def down(i, m, q):
                for w in range(2):
                    e = pe.value_load(table[0:1, bass.ds(i * 2 + w, 1)], min_val=0, max_val=E - 1)
                    if w == 0:
                        need(pe, "hidT", i)
                        freed(pe, "ye", i, 2, 2)
                    last = mm(ps8[6 + m % 2][:, w * D:(w + 1) * D], hidT[:, m % 2, w * I:(w + 1) * I],
                              wdn[:, bass.ds(e * D, D)], start=True, stop=True)
                last.then_inc(S_["ye_ps"], 1)

            def pstep(tile):
                at_tile(tile, -1, tr_xe)
                at_tile(tile, 0, gate_up)
                at_tile(tile, 1, tr_hid)
                at_tile(tile, 2, down)
            over_pairs(pe, pstep)

            for one in xn2T_st:
                pe.wait_ge(one, 16 * NT // 2)

            def s_up(s):
                xs = store[:, s * B * D:(s + 1) * B * D].rearrange("p (b k n) -> p k b n", b=B, k=KT)
                for h in range(2):
                    if s >= 1:
                        pe.wait_ge(S_["shh"], 2 * (s - 1) + h + 1)
                    elif h == 0:
                        need(pe, "ye", NPR - 1, 2)
                    for g in range(2):
                        for k in range(KT):
                            last = mm(ps8[2 * h + g].rearrange("p (b n) -> p b n", b=B),
                                      wsgu[:, k, g * SI + h * P:g * SI + (h + 1) * P],
                                      xs[:, k, :, :], start=k == 0, stop=k == KT - 1)
                    last.then_inc(S_["sg_ps"], 1)

            def s_down(s):
                need(pe, "shh", s, 2)
                for b in range(B):
                    if s >= 1:
                        pe.wait_ge(S_["outb"], B * (s - 1) + b + 1)
                    for k in range(KT):
                        last = mm(ps8[4 + b][:, 0:D], shh[:, (s % 2) * 2 + k, b * P:(b + 1) * P], wsdn[:, k, :],
                                  start=k == 0, stop=k == KT - 1)
                    last.then_inc(S_["sy_ps"], 1)
            for s in range(SB + 1):
                if s < SB:
                    s_up(s)
                if s >= 1:
                    s_down(s - 1)

        @block.vector
        def _(v):
            tt, ts, red = v.tensor_tensor, v.tensor_scalar, v.tensor_reduce

            for s in range(SB):
                v.wait_ge(ld_x[s], 16)
                for b in range(B):
                    t = s * B + b
                    last = v.bn_stats(stats1[:, t, :], store[:, t * D:(t + 1) * D])
            last.then_inc(S_["stats1_ready"], 1)
            v.wait_ge(S_["stats1_ready"], 1)
            me, mo = stats1[:, :, 1], stats1[:, :, 4]
            ve, vo = stats1[:, :, 2], stats1[:, :, 5]
            tt(mean1[:, :], me, mo, ALU.add).then_inc(S_["mean1_ready"], 1)
            tt(tmp1[:, 0, :], me, mo, ALU.subtract).then_inc(S_["tmp_ready"], 1)
            tt(tmp1[:, 1, :], ve, vo, ALU.add).then_inc(S_["tmp_ready"], 1)
            v.wait_ge(S_["tmp_ready"], 2)
            tt(tmp1[:, 0, :], tmp1[:, 0, :], tmp1[:, 0, :], ALU.mult).then_inc(S_["tmp_ready"], 1)
            ts(tmp1[:, 1, :], tmp1[:, 1, :], 1.0 / D, EPS, ALU.mult, ALU.add).then_inc(S_["tmp_ready"], 1)
            v.wait_ge(S_["mean1_ready"], 1)
            ts(mean1[:, :], mean1[:, :], 0.5, None, ALU.mult).then_inc(S_["mean1_ready"], 1)
            v.wait_ge(S_["tmp_ready"], 4)
            v.scalar_tensor_tensor(tmp1[:, 0, :], tmp1[:, 0, :], 0.25, tmp1[:, 1, :], ALU.mult,
                                   ALU.add).then_inc(S_["var1_ready"], 1)

            v.wait_ge(S_["ld_const"], 32)
            v.tensor_copy(repb[:, :], const("rep")[0:C, :]).then_inc(S_["repb_ready"], 1)
            v.tensor_copy(trib[:, :], const("tri")).then_inc(S_["repb_ready"], 1)
            v.tensor_copy(onesb[:, :], const("ones")).then_inc(S_["repb_ready"], 1)
            v.wait_ge(S_["ld_mask"], 16)
            ts(maskb[:, :], maskw[0:C, :], 0.0, MASKED, ALU.is_equal, ALU.mult).then_inc(S_["mask_ready"], 1)
            v.wait_ge(S_["mask_ready"], 1)
            v.wait_ge(S_["ld_w"], 16 * W_LOADS)
            hi, mid, lo = (bo_p[0:3, i * P:(i + 1) * P].bitcast(bf16) for i in range(3))
            f, r, acc3 = bo_f[0:3, :], bo_r[0:3, :], bo_s[0:3, :]
            third = const("third")
            steps = (lambda: v.tensor_copy(hi, f),
                     lambda: tt(r, f, hi, ALU.subtract),
                     lambda: v.tensor_copy(mid, r),
                     lambda: tt(r, r, mid, ALU.subtract),
                     lambda: v.tensor_copy(lo, r),
                     lambda: ts(acc3, hi, third[0:3, 0:1], None, ALU.mult),
                     lambda: v.scalar_tensor_tensor(acc3, mid, third[0:3, 1:2], acc3, ALU.mult, ALU.add),
                     lambda: v.scalar_tensor_tensor(acc3, lo, third[0:3, 2:3], acc3, ALU.mult, ALU.add),
                     lambda: v.tensor_copy(bo3[:, :], acc3))
            for i, one in enumerate(steps):
                one().then_inc(S_["bo_parts"], 1)
                v.wait_ge(S_["bo_parts"], i + 1)
            v.nop().then_inc(S_["wg_free"], 1)
            need(v, "k_ps", 0)
            for h in range(2):
                for sub in range(2):
                    last = ts(kbd[:, h, :, sub * C:(sub + 1) * C],
                              ps8[4 + h][:, 0:B * C].rearrange("p (b c) -> p b c", b=B),
                              bias_qk[:, 2 + h:3 + h], const("submask")[:, sub:sub + 1], ALU.add, ALU.mult)
                last.then_inc(S_["kbd_ready"], 1)
            for b in range(B):
                need(v, "v_ps", b)
                vm = const("vmask").rearrange("p (c j) -> p c j", c=NCH)
                tt(vbd[:, b, :, :, 0:DH].rearrange("p c j d -> p (c j) d"),
                   ps8[b][:, 0:NCH * 48].rearrange("p (c d) -> p c d", d=DH),
                   const("vmask").unsqueeze(2).broadcast_to([P, NCH * 3, DH]), ALU.mult)
                v.tensor_copy(vbd[:, b, :, :, DH], vm).then_inc(S_["vbd_ready"], 1)
            need(v, "gb_ps", 0)
            v.tensor_copy(gbias[:, :], bank[2][:, 0:E]).then_inc(S_["gb_ready"], 1)
            need(v, "rstd1_ready", 0)
            v.wait_ge(S_["mean1_ready"], 2)
            v.scalar_tensor_tensor(shift1[:, :], mean1[:, :], -1.0, rstd1[:, :], ALU.mult,
                                   ALU.mult).then_inc(S_["norm1_ready"], 1)
            need(v, "gb_ready", 0)
            need(v, "probs_zero", 0)

            mx4 = mx[:, :].rearrange("p (r h) -> p r h", r=4)

            def four(half):
                return sc_ps[:, 2 * half:2 * half + 2, 0:HCOLS].rearrange("p r (h c) -> p r h c", h=4)

            def row_max(half):
                def stage(t, m, s):
                    if half == 0:
                        need(v, "scores", t)
                    red(mx4[:, 2 * half:2 * half + 2, :], four(half), AX.X, ALU.max).then_inc(S_[f"score_max{half}"], 1)
                return stage

            def shift(half):
                def stage(t, m, s):
                    need(v, f"score_max{half}", t)
                    if half == 0:
                        freed(v, "pT_ps2", t, 2)
                    last = tt(probs[:, m % 2, 0:HC].rearrange("p (r h c) -> p r h c", r=4, h=4)[:, 2 * half:2 * half + 2],
                              four(half), mx4[:, 2 * half:2 * half + 2, :].unsqueeze(3).broadcast_to([P, 2, 4, C]),
                              ALU.subtract)
                    if half == 1:
                        last.then_inc(S_["score_sub"], 1)
                return stage

            pvv = pv_ps.rearrange("p (h n) -> p h n", h=H)

            def inverse_sums(t, m, s):
                need(v, "pv", t)
                v.reciprocal(rsum[:, :], pvv[:, :, DH]).then_inc(S_["o_rcp"], 1)

            def normalise(t, m, s):
                need(v, "o_rcp", t)
                freed(v, "oT_ps", t, 2)
                tt(o[:, m % 2, :].rearrange("p (h n) -> p h n", h=H), pvv[:, :, 0:DH],
                   rsum[:, :].unsqueeze(2).broadcast_to([P, H, DH]), ALU.mult).then_inc(S_["o"], 1)

            def residual(t, m, s):
                need(v, "y_ps", t)
                stored(v, x1_st, m, s)
                tt(x1[:, m % 2, :], y_ps, store[:, bass.ds(t * D, D)], ALU.add).then_inc(S_["x1"], 1)

            def x1_stats(t, m, s):
                need(v, "x1", t)
                v.bn_stats(stats2[:, :], x1[:, m % 2, :]).then_inc(S_["stats2"], 1)

            def x1_mean_var(t, m, s):
                need_apart(v, "stats2", t)
                v.bn_aggr(mv2[:, m % 2, :], stats2[:, :]).then_inc(S_["mv2"], 1)

            def x1_var_eps(t, m, s):
                need(v, "mv2", t)
                freed(v, "rstd2", t, 2)
                ts(var2[:, m % 2:m % 2 + 1], mv2[:, m % 2, 1:2], EPS, None, ALU.add).then_inc(S_["var2"], 1)

            def norm2(t, m, s):
                need(v, "rstd2", t)
                stored(v, scat, m, s)
                ts(rowb[:, m, 0:D], x1[:, m % 2, :], mv2[:, m % 2, 0:1], rstd2[:, m % 2:m % 2 + 1],
                   ALU.subtract, ALU.mult).then_inc(S_["xn2"], 1)

            iota = const("iota")

            def gate_add(t, m, s):
                need(v, "gate_exp", t)
                ts(gsum[:, :], gexp[:, m % 2, :], 1.0, None, ALU.add).then_inc(S_["gate_add"], 1)

            def sigmoid(t, m, s):
                need(v, "gate_add", t)
                v.reciprocal(score[:, :], gsum[:, :]).then_inc(S_["score"], 1)

            def corrected(t, m, s):
                need(v, "score", t)
                tt(sfc[:, :], score[:, :], gbias[:, :], ALU.add).then_inc(S_["sfc"], 1)

            def group_max(t, m, s):
                need(v, "sfc", t)
                red(gmax[:, :], sfc[:, :].rearrange("p (g n) -> p g n", g=NG), AX.X, ALU.max).then_inc(S_["gmax"], 1)

            def group_top(t, m, s):
                need_apart(v, "gmax", t)
                v.max(gtop[:, :], gmax[:, :]).then_inc(S_["gtop"], 1)

            def group_index(t, m, s):
                need_apart(v, "gtop", t)
                v.max_index(gidx[:, :], gtop[:, :], gmax[:, :]).then_inc(S_["gidx"], 1)

            def group_onehot(t, m, s):
                need(v, "gidx", t)
                tt(ghot[:, :, :], iota[:, 0:NG].unsqueeze(2).broadcast_to([P, NG, TOPG]),
                   gidx[:, 0:TOPG].unsqueeze(1).broadcast_to([P, NG, TOPG]), ALU.is_equal).then_inc(S_["ghot"], 1)

            def group_select(t, m, s):
                need(v, "ghot", t)
                red(gsel[:, :], ghot[:, :, :], AX.X, ALU.add).then_inc(S_["gsel"], 1)

            def mask_groups(t, m, s):
                need(v, "gsel", t)
                tt(masked[:, :].rearrange("p (g n) -> p g n", g=NG), sfc[:, :].rearrange("p (g n) -> p g n", g=NG),
                   gsel[:, :].unsqueeze(2).broadcast_to([P, NG, GS]), ALU.mult).then_inc(S_["masked"], 1)

            def expert_top(t, m, s):
                need_apart(v, "masked", t)
                v.max(etop[:, :], masked[:, :]).then_inc(S_["etop"], 1)

            def expert_index(t, m, s):
                need_apart(v, "etop", t)
                v.max_index(eidx[:, :], etop[:, :], masked[:, :]).then_inc(S_["eidx"], 1)

            def expert_onehot(t, m, s):
                need(v, "eidx", t)
                tt(ehot[:, :, :], iota.unsqueeze(2).broadcast_to([P, E, TOPK]),
                   eidx[:, 0:TOPK].unsqueeze(1).broadcast_to([P, E, TOPK]), ALU.is_equal).then_inc(S_["ehot"], 1)

            def expert_select(t, m, s):
                need(v, "ehot", t)
                red(sel[:, :], ehot[:, :, :], AX.X, ALU.max).then_inc(S_["sel"], 1)

            def chosen_scores(t, m, s):
                need(v, "sel", t)
                v.scalar_tensor_tensor(wsel[:, :], sel[:, :], 1.0, score[:, :], ALU.mult, ALU.mult,
                                       accum_out=wsum[:, 0:1]).then_inc(S_["wsel"], 1)

            def sum_guard(t, m, s):
                need(v, "wsel", t)
                ts(wsum[:, 1:2], wsum[:, 0:1], 1e-20, None, ALU.add).then_inc(S_["wsum_e"], 1)

            def sum_inverse(t, m, s):
                need(v, "wsum_e", t)
                v.reciprocal(wsum[:, 2:3], wsum[:, 1:2]).then_inc(S_["wsum_r"], 1)

            def row_weights(t, m, s):
                need(v, "wsum_r", t)
                ts(rowb[:, m, D:D + E], wsel[:, :], wsum[:, 2:3], ROUTE_SCALE, ALU.mult,
                   ALU.mult).then_inc(S_["row_w"], 1)

            def place_all(t, m, s):
                need(v, "rank", t)
                tt(place[:, :], rk_ps, const("region"), ALU.add).then_inc(S_["place"], 1)

            def count_on(t, m, s):
                tt(selcum[:, :], selcum[:, :], sel[:, :], ALU.add).then_inc(S_["selcum"], 1)

            def place_chosen(t, m, s):
                need(v, "place", t)
                tt(placek[:, :, :], ehot[:, :, :].rearrange("p e k -> p k e"),
                   place[:, :].unsqueeze(1).broadcast_to([P, TOPK, E]), ALU.mult).then_inc(S_["placek"], 1)

            def place_index(t, m, s):
                need(v, "placek", t)
                dest_free(v, m, s)
                with nc.allow_low_precision(reason="whole numbers below 2**24"):
                    red(dest[:, m % 2, 0:TOPK], placek[:, :, :], AX.X, ALU.add).then_inc(S_["dest"], 1)

            def step(tile):
                at_tile(tile, 3, residual)
                at_tile(tile, 5, chosen_scores)
                at_tile(tile, 4, gate_add)
                at_tile(tile, 3, x1_stats)
                at_tile(tile, 5, sum_guard)
                at_tile(tile, 4, sigmoid)
                at_tile(tile, 5, sum_inverse)
                at_tile(tile, 3, x1_mean_var)
                at_tile(tile, 2, inverse_sums)
                at_tile(tile, 5, row_weights)
                at_tile(tile, 3, x1_var_eps)
                at_tile(tile, 4, corrected)
                at_tile(tile, 5, place_all)
                at_tile(tile, 5, count_on)
                at_tile(tile, 4, group_max)
                at_tile(tile, 2, normalise)
                at_tile(tile, 4, group_top)
                at_tile(tile, 5, place_chosen)
                at_tile(tile, 4, group_index)
                at_tile(tile, 3, norm2)
                at_tile(tile, 4, group_onehot)
                at_tile(tile, 5, place_index)
                at_tile(tile, 4, group_select)
                at_tile(tile, 0, row_max(0))
                at_tile(tile, 4, mask_groups)
                at_tile(tile, 0, row_max(1))
                at_tile(tile, 4, expert_top)
                at_tile(tile, 0, shift(0))
                at_tile(tile, 4, expert_index)
                at_tile(tile, 4, expert_onehot)
                at_tile(tile, 4, expert_select)
                at_tile(tile, 0, shift(1))
            over_tiles(v, step)

            need(v, "counts", 0)
            v.tensor_copy(cnt[:, :], rk_ps).then_inc(S_["cnt"], 1)
            need(v, "cnt", 0)
            tt(tails[0:1, :], cnt[0:1, :], const("region")[0:1, :], ALU.add).then_inc(S_["tail_rows"], 1)
            cmp = pTf[:, 0:E * E].rearrange("p (a b) -> p a b", a=E)
            ts(blkcum[:, :], const("iota"), float(P), None, ALU.mult).then_inc(S_["sch_a"], 1)
            v.wait_ge(S_["sch_a"], 1)
            tt(cmp, cnt[:, :].unsqueeze(2).broadcast_to([P, E, E]),
               blkcum[:, :].unsqueeze(1).broadcast_to([P, E, E]), ALU.is_gt).then_inc(S_["sch_a"], 1)
            v.wait_ge(S_["sch_a"], 2)
            red(blocks[:, :], cmp, AX.X, ALU.add).then_inc(S_["sch_a"], 1)
            v.wait_ge(S_["sch_a"], 3)
            tt(cmp, const("iota").unsqueeze(2).broadcast_to([P, E, E]),
               const("iota").unsqueeze(1).broadcast_to([P, E, E]), ALU.is_ge).then_inc(S_["sch_a"], 1)
            v.wait_ge(S_["sch_a"], 4)
            tt(cmp, cmp, blocks[:, :].unsqueeze(1).broadcast_to([P, E, E]), ALU.mult).then_inc(S_["sch_a"], 1)
            v.wait_ge(S_["sch_a"], 5)
            red(blkcum[:, :], cmp, AX.X, ALU.add).then_inc(S_["sch_b"], 1)
            v.wait_ge(S_["sch_b"], 1)
            le = cmp[:, 0:2, :]
            jt = const("jtile")
            tt(le, blkcum[:, :].unsqueeze(1).broadcast_to([P, 2, E]), jt.unsqueeze(2).broadcast_to([P, 2, E]),
               ALU.is_le).then_inc(S_["sch_c"], 1)
            v.wait_ge(S_["sch_c"], 1)
            red(sched[:, 0:2], le, AX.X, ALU.add).then_inc(S_["sch_c"], 1)
            tt(cmp[:, 2:4, :], le, blocks[:, :].unsqueeze(1).broadcast_to([P, 2, E]), ALU.mult).then_inc(S_["sch_c"], 1)
            v.wait_ge(S_["sch_c"], 3)
            red(sched[:, 2:4], cmp[:, 2:4, :], AX.X, ALU.add).then_inc(S_["sch_d"], 1)
            v.wait_ge(S_["sch_d"], 1)
            tt(sched[:, 2:4], jt, sched[:, 2:4], ALU.subtract).then_inc(S_["sch_d"], 1)
            v.wait_ge(S_["sch_d"], 2)
            ts(sched[:, 2:4], sched[:, 2:4], float(P), None, ALU.mult).then_inc(S_["sch_d"], 1)
            v.wait_ge(S_["sch_d"], 3)
            v.scalar_tensor_tensor(sched[:, 2:4], sched[:, 0:2], float(REGION), sched[:, 2:4], ALU.mult,
                                   ALU.add).then_inc(S_["sch_d"], 1)
            v.wait_ge(S_["sch_d"], 4)
            ts(sched2[:, 2:4], sched[:, 2:4], float(PAD_ROW), None, ALU.min)
            ts(sched2[:, 0:2], sched[:, 0:2], float(E - 1), None, ALU.min).then_inc(S_["sch_e"], 1)
            need(v, "sch_ps", 0)
            v.tensor_copy(table[:, :], bank[3][0:1, :]).then_inc(S_["table"], 1)
            need(v, "table", 0)

            def hidden(i, m, q):
                need(v, "act", i)
                freed(v, "hidT_ps", i, 2)
                tt(hid[:, m % 2, :].rearrange("p (w n) -> p w n", w=2), act[:, m % 2, :].rearrange("p (w n) -> p w n", w=2),
                   ps8[2 + m % 2].rearrange("p (w n) -> p w n", w=2)[:, :, I:2 * I], ALU.mult).then_inc(S_["hid"], 1)

            def ev_hidT(i, m, q):
                need(v, "hidT_ps", i)
                freed(v, "ye_ps", i, 2)
                v.tensor_copy(hidT[:, m % 2, :], ps8[4 + m % 2][:, 0:2 * I]).then_inc(S_["hidT"], 1)

            def weigh(i, m, q):
                for w in range(2):
                    e = v.value_load(table[0:1, bass.ds(i * 2 + w, 1)], min_val=0, max_val=E - 1)
                    if w == 0:
                        need(v, "ye_ps", i)
                    r, c = (2 * m + w) % R_ACC, q * (2 * UB // R_ACC) + (2 * m + w) // R_ACC
                    if not (isinstance(c, int) and c == 0):
                        v.wait_ge(acc_add[r], c * 16)
                    ts(ye[:, r, :], ps8[6 + m % 2][:, w * D:(w + 1) * D], xe[:, 2 * m + w, bass.ds(e + D, 1)], None,
                       ALU.mult).then_inc(S_["ye"], 1)

            def pstep(tile):
                at_tile(tile, 0, hidden)
                at_tile(tile, 1, ev_hidT)
                at_tile(tile, 2, weigh)
            over_pairs(v, pstep)

            def s_hidden(s):
                for h in range(2):
                    v.wait_ge(S_["shg"], 2 * s + h + 1)
                    if s >= 2:
                        need(v, "sy_ps", s - 2, B)
                    tt(shh[:, (s % 2) * 2 + h, :], shg[:, h, :], ps8[2 * h + 1], ALU.mult).then_inc(S_["shh"], 1)

            def s_sum(s):
                v.wait_ge(ld_acc[s % 2], 16 * R_ACC * (s // 2 + 1))
                a0 = acc_in[:, (s % 2) * R_ACC, :]
                for r in range(1, R_ACC):
                    tt(a0, a0, acc_in[:, (s % 2) * R_ACC + r, :], ALU.add).then_inc(S_["acc_sum"], 1)
                    v.wait_ge(S_["acc_sum"], s * (R_ACC - 1) + r)
                if s >= 2:
                    v.wait_ge(S_["out_st"], 16 * (s - 1))
                for b in range(B):
                    v.wait_ge(S_["sy_ps"], s * B + b + 1)
                    tt(outb[:, s % 2, b * D:(b + 1) * D], ps8[4 + b][:, 0:D], a0[:, b * D:(b + 1) * D],
                       ALU.add).then_inc(S_["outb"], 1)
            for s in range(SB + 1):
                if s < SB:
                    s_hidden(s)
                if s >= 1:
                    s_sum(s - 1)


def kernel(x, ctx_1024, mask_SxS2_ik0, L0_xattn_Wq, L0_xattn_bq, L0_xattn_Wk, L0_xattn_bk, L0_xattn_Wv, L0_xattn_bv,
           L0_xattn_Wo, L0_xattn_bo, L0_ffn_gate_weight, L0_ffn_e_score_correction_bias, L0_ffn_experts_gate_up,
           L0_ffn_experts_down, L0_ffn_shared_gate_w, L0_ffn_shared_up_w, L0_ffn_shared_down_w):
    import concourse.bacc as bacc
    from concourse.bass_utils import run_bass_kernel_spmd

    order = np.array([(4 * r + 2 * h + sub) * DH + d
                      for h in range(2) for r in range(4) for sub in range(2) for d in range(DH)])
    wq, wk = np.asarray(L0_xattn_Wq).T[:, order], np.asarray(L0_xattn_Wk).T[:, order]
    bq, bk = (np.asarray(b)[order].reshape(2, P).T for b in (L0_xattn_bq, L0_xattn_bk))
    const, ids = constants()
    arrays = {
        "x": x, "mask": np.asarray(mask_SxS2_ik0).T, "wq": wq, "wk": wk,
        "wv": np.asarray(L0_xattn_Wv).T, "wo": np.asarray(L0_xattn_Wo).T,
        "bqk": np.concatenate([bq, bk], 1), "bvo": np.stack([L0_xattn_bv, L0_xattn_bo]),
        "ctx_t": np.asarray(ctx_1024).transpose(0, 2, 1),
        "gate_w": np.asarray(L0_ffn_gate_weight).T, "gate_b": L0_ffn_e_score_correction_bias,
        "egu": np.asarray(L0_ffn_experts_gate_up).transpose(0, 2, 1),
        "edn": np.asarray(L0_ffn_experts_down).transpose(0, 2, 1),
        "sgu": np.concatenate([np.asarray(L0_ffn_shared_gate_w).T, np.asarray(L0_ffn_shared_up_w).T], 1),
        "sdn": np.asarray(L0_ffn_shared_down_w).T, "const": const, "ids": ids,
    }
    arrays = {f"in_{n}": np.ascontiguousarray(a) for n, a in arrays.items()}
    nc = bacc.Bacc("TRN2", target_bir_lowering=False, num_devices=1)
    aps = [nc.dram_tensor(n, a.shape, mybir.dt.from_np(a.dtype), kind="ExternalInput").ap() for n, a in arrays.items()]
    out = nc.dram_tensor("out", (B, S, D), mybir.dt.float32, kind="ExternalOutput").ap()
    build(nc, *aps, out)
    return run_bass_kernel_spmd(nc, [arrays], core_ids=[0]).results[0]["out"]
```
